# Optimizing a Trainium2 kernel written in Bass

```python
import numpy as np
import jax
import jax.numpy as jnp

def _softmax(x, axis=-1):
    return jax.nn.softmax(x, axis=axis)

def _gelu(x):
    return jax.nn.gelu(x, approximate=True)

def _silu(x):
    return jax.nn.silu(x)

def _sigmoid(x):
    return jax.nn.sigmoid(x)

def _layernorm(x, axis=-1, eps=1e-05):
    m = jnp.mean(x, axis=axis, keepdims=True)
    v = jnp.var(x, axis=axis, keepdims=True)
    return (x - m) / jnp.sqrt(v + eps)

def _scatter_add(tgt, idx, src, axis=0):
    return tgt.at[idx].add(src)

def _segment_sum(src, seg, n):
    return jax.ops.segment_sum(src, seg, n)
kernel_name = 'mk_decoder_postln_d1_seqx_r8_faa8b7'

def setup_inputs(seed: int=0):
    np.random.seed(seed)
    _w = jnp.asarray

    def _rec_inputs():
        import jax
        import jax.numpy as jnp
        _rk = jax.random.key(seed)
        x = -0.0002928 + 1 * jax.random.normal(jax.random.fold_in(_rk, 1), (8, 256, 128), jnp.float32)
        _lenS = 256 - jax.random.randint(jax.random.fold_in(_rk, 7), (8,), 0, max(1, 256 // 4) + 1, jnp.int32)
        _lenS2 = 256 - jax.random.randint(jax.random.fold_in(_rk, 8), (8,), 0, max(1, 256 // 4) + 1, jnp.int32)
        _ctx_1024P = jax.random.normal(jax.random.fold_in(_rk, 11), (8, 16, 128), jnp.float32)
        _ctx_1024c = jax.random.dirichlet(jax.random.fold_in(_rk, 511), 0.3 * jnp.ones((16,), jnp.float32), (8, 256))
        _ctx_1024t = jnp.einsum('bsk,bkd->bsd', _ctx_1024c, _ctx_1024P)
        _ctx_1024t = _ctx_1024t * jax.lax.rsqrt(jnp.mean(jnp.square(_ctx_1024t)) + 1e-12) * 0.953939
        ctx_1024 = -1.39393e-06 + 0.999914 * (_ctx_1024t + 0.3 * jax.random.normal(jax.random.fold_in(_rk, 611), (8, 256, 128), jnp.float32))
        return (x, ctx_1024)
    x, ctx_1024 = _rec_inputs()

    def _L0_attn_setup():
        import jax, jax.numpy as jnp
        import numpy as np
        DIM = 128
        D_STATE = 32
        HEADDIM = 64
        EXPAND = 2
        CHUNK = 64
        D_INNER = EXPAND * DIM
        NHEADS = D_INNER // HEADDIM
        ROPE_DIM = int(0.5 * D_STATE)
        D_IN_PROJ = 2 * D_INNER + 2 * D_STATE + NHEADS
        B_SZ = 4
        L = 512

        def _segsum(a):
            T = a.shape[-1]
            cs = jnp.cumsum(a, axis=-1)
            d = cs[..., :, None] - cs[..., None, :]
            mask = jnp.tril(jnp.ones((T, T), bool))
            return jnp.where(mask, d, -jnp.inf)

        def _rope(v):
            t = jnp.arange(v.shape[1], dtype=jnp.float32)
            inv_freq = 1.0 / 10000.0 ** (jnp.arange(0, ROPE_DIM, 2, dtype=jnp.float32) / ROPE_DIM)
            ang = t[:, None] * inv_freq[None, :]
            cos, sin = (jnp.cos(ang)[None], jnp.sin(ang)[None])
            vr, vp = (v[..., :ROPE_DIM], v[..., ROPE_DIM:])
            v1, v2 = (vr[..., 0::2], vr[..., 1::2])
            r = jnp.stack([v1 * cos - v2 * sin, v1 * sin + v2 * cos], axis=-1)
            return jnp.concatenate([r.reshape(vr.shape), vp], axis=-1)
        key = jax.random.key(seed)
        ks = jax.random.split(key, 8)
        return {'x': jax.random.normal(ks[0], (B_SZ, L, DIM), jnp.float32), 'ln_w': jnp.ones((DIM,), jnp.float32), 'ln_b': jnp.zeros((DIM,), jnp.float32), 'W_in': jax.random.normal(ks[1], (DIM, D_IN_PROJ), jnp.float32) * 0.02, 'dt_bias': jax.random.uniform(ks[2], (NHEADS,), jnp.float32, -4.0, -1.0), 'A_log': jnp.log(jax.random.uniform(ks[3], (NHEADS,), jnp.float32, 1.0, 16.0)), 'D': jax.random.normal(ks[4], (NHEADS,), jnp.float32) * 0.1 + 1.0, 'rms_w': jnp.ones((D_INNER,), jnp.float32), 'W_out': jax.random.normal(ks[5], (D_INNER, DIM), jnp.float32) * 0.02}
    _L0_attn_all = _L0_attn_setup()
    _L0_attn_in = {k: v for k, v in _L0_attn_all.items() if k in ('ln_w', 'ln_b', 'W_in', 'dt_bias', 'A_log', 'D', 'rms_w', 'W_out')}
    del _L0_attn_all

    def _L0_xattn_setup():
        import jax, jax.numpy as jnp
        import numpy as np
        D_MODEL = 128
        NUM_HEAD = 16
        key = jax.random.key(seed)
        ks = jax.random.split(key, 11)
        B, S, D = (2, 256, D_MODEL)
        s = 0.02
        return {'Q': jax.random.normal(ks[0], (B, S, D), jnp.float32), 'K': jax.random.normal(ks[1], (B, S, D), jnp.float32), 'V': jax.random.normal(ks[2], (B, S, D), jnp.float32), 'Wq': jax.random.normal(ks[3], (D, D), jnp.float32) * s, 'bq': jnp.zeros((D,), jnp.float32), 'Wk': jax.random.normal(ks[4], (D, D), jnp.float32) * s, 'bk': jnp.zeros((D,), jnp.float32), 'Wv': jax.random.normal(ks[5], (D, D), jnp.float32) * s, 'bv': jnp.zeros((D,), jnp.float32), 'Wo': jax.random.normal(ks[6], (D, D), jnp.float32) * s, 'bo': jnp.zeros((D,), jnp.float32)}
    _L0_xattn_all = _L0_xattn_setup()
    _L0_xattn_in = {k: v for k, v in _L0_xattn_all.items() if k in ('Wq', 'bq', 'Wk', 'bk', 'Wv', 'bv', 'Wo', 'bo')}
    del _L0_xattn_all

    def _L0_ffn_setup():
        import jax, jax.numpy as jnp
        import numpy as np
        E = 8
        TOPK = 2
        D = 128
        F = 512
        B, S = (2, 64)

        def _gmm(x, W, expert_onehot):
            return jnp.einsum('te,td,edf->tf', expert_onehot, x, W)
        key = jax.random.key(seed)
        k1, k2, k3, k4, k5 = jax.random.split(key, 5)
        scale_d = 1.0 / np.sqrt(D)
        scale_f = 1.0 / np.sqrt(F)
        return {'inputs': jax.random.normal(k1, (B, S, D), jnp.float32), 'gate_kernel': jax.random.normal(k2, (D, E), jnp.float32) * scale_d, 'w0': jax.random.normal(k3, (E, D, F), jnp.float32) * scale_d, 'w1': jax.random.normal(k4, (E, D, F), jnp.float32) * scale_d, 'wo': jax.random.normal(k5, (E, F, D), jnp.float32) * scale_f}
    _L0_ffn_all = _L0_ffn_setup()
    _L0_ffn_in = {k: v for k, v in _L0_ffn_all.items() if k in ('gate_kernel', 'w0', 'w1', 'wo')}
    del _L0_ffn_all
    return {'x': x, 'ctx_1024': ctx_1024, 'L0_attn_ln_w': _L0_attn_in['ln_w'], 'L0_attn_ln_b': _L0_attn_in['ln_b'], 'L0_attn_W_in': _L0_attn_in['W_in'], 'L0_attn_dt_bias': _L0_attn_in['dt_bias'], 'L0_attn_A_log': _L0_attn_in['A_log'], 'L0_attn_D': _L0_attn_in['D'], 'L0_attn_rms_w': _L0_attn_in['rms_w'], 'L0_attn_W_out': _L0_attn_in['W_out'], 'L0_xattn_Wq': _L0_xattn_in['Wq'], 'L0_xattn_bq': _L0_xattn_in['bq'], 'L0_xattn_Wk': _L0_xattn_in['Wk'], 'L0_xattn_bk': _L0_xattn_in['bk'], 'L0_xattn_Wv': _L0_xattn_in['Wv'], 'L0_xattn_bv': _L0_xattn_in['bv'], 'L0_xattn_Wo': _L0_xattn_in['Wo'], 'L0_xattn_bo': _L0_xattn_in['bo'], 'L0_ffn_gate_kernel': _L0_ffn_in['gate_kernel'], 'L0_ffn_w0': _L0_ffn_in['w0'], 'L0_ffn_w1': _L0_ffn_in['w1'], 'L0_ffn_wo': _L0_ffn_in['wo']}

def reference(x, ctx_1024, L0_attn_ln_w, L0_attn_ln_b, L0_attn_W_in, L0_attn_dt_bias, L0_attn_A_log, L0_attn_D, L0_attn_rms_w, L0_attn_W_out, L0_xattn_Wq, L0_xattn_bq, L0_xattn_Wk, L0_xattn_bk, L0_xattn_Wv, L0_xattn_bv, L0_xattn_Wo, L0_xattn_bo, L0_ffn_gate_kernel, L0_ffn_w0, L0_ffn_w1, L0_ffn_wo):
    import jax
    import jax.numpy as jnp

    def _L0_attn_ref(x, ln_w, ln_b, W_in, dt_bias, A_log, D, rms_w, W_out):
        import jax, jax.numpy as jnp
        import numpy as np
        DIM = 128
        D_STATE = 32
        HEADDIM = 64
        EXPAND = 2
        CHUNK = 64
        D_INNER = EXPAND * DIM
        NHEADS = D_INNER // HEADDIM
        ROPE_DIM = int(0.5 * D_STATE)
        D_IN_PROJ = 2 * D_INNER + 2 * D_STATE + NHEADS
        B_SZ = 4
        L = 512

        def _segsum(a):
            T = a.shape[-1]
            cs = jnp.cumsum(a, axis=-1)
            d = cs[..., :, None] - cs[..., None, :]
            mask = jnp.tril(jnp.ones((T, T), bool))
            return jnp.where(mask, d, -jnp.inf)

        def _rope(v):
            t = jnp.arange(v.shape[1], dtype=jnp.float32)
            inv_freq = 1.0 / 10000.0 ** (jnp.arange(0, ROPE_DIM, 2, dtype=jnp.float32) / ROPE_DIM)
            ang = t[:, None] * inv_freq[None, :]
            cos, sin = (jnp.cos(ang)[None], jnp.sin(ang)[None])
            vr, vp = (v[..., :ROPE_DIM], v[..., ROPE_DIM:])
            v1, v2 = (vr[..., 0::2], vr[..., 1::2])
            r = jnp.stack([v1 * cos - v2 * sin, v1 * sin + v2 * cos], axis=-1)
            return jnp.concatenate([r.reshape(vr.shape), vp], axis=-1)
        B, Ls, _ = x.shape
        mu = jnp.mean(x, -1, keepdims=True)
        var = jnp.var(x, -1, keepdims=True)
        h = (x - mu) * jax.lax.rsqrt(var + 1e-06) * ln_w + ln_b
        zxbcdt = h @ W_in
        z = zxbcdt[..., :D_INNER]
        xs = jax.nn.silu(zxbcdt[..., D_INNER:2 * D_INNER])
        Bc = jax.nn.silu(zxbcdt[..., 2 * D_INNER:2 * D_INNER + D_STATE])
        Cc = jax.nn.silu(zxbcdt[..., 2 * D_INNER + D_STATE:2 * D_INNER + 2 * D_STATE])
        dt = jax.nn.softplus(zxbcdt[..., -NHEADS:] + dt_bias)
        Bc, Cc = (_rope(Bc), _rope(Cc))
        A = -jnp.exp(A_log)
        xh = xs.reshape(B, Ls, NHEADS, HEADDIM)
        nc = Ls // CHUNK
        Xc = (xh * dt[..., None]).reshape(B, nc, CHUNK, NHEADS, HEADDIM)
        a = (dt * A).reshape(B, nc, CHUNK, NHEADS).transpose(0, 3, 1, 2)
        Bk = Bc.reshape(B, nc, CHUNK, D_STATE)
        Ck = Cc.reshape(B, nc, CHUNK, D_STATE)
        A_cs = jnp.cumsum(a, axis=-1)
        Lmat = jnp.exp(_segsum(a))
        scores = jnp.einsum('bcln,bcsn->bcls', Ck, Bk)
        M = scores[:, None] * Lmat
        Yd = jnp.einsum('bhcls,bcshp->bclhp', M, Xc)
        decay_states = jnp.exp(A_cs[..., -1:] - A_cs)
        states = jnp.einsum('bcln,bhcl,bclhp->bchpn', Bk, decay_states, Xc)
        states = jnp.concatenate([jnp.zeros_like(states[:, :1]), states], axis=1)
        dc = jnp.exp(_segsum(jnp.pad(A_cs[..., -1], ((0, 0), (0, 0), (1, 0)))))
        states_in = jnp.einsum('bhzc,bchpn->bzhpn', dc, states)[:, :-1]
        Yo = jnp.einsum('bcln,bchpn,bhcl->bclhp', Ck, states_in, jnp.exp(A_cs))
        y = (Yd + Yo).reshape(B, Ls, NHEADS, HEADDIM) + xh * D[None, None, :, None]
        y = y.reshape(B, Ls, D_INNER)
        y = y * jax.nn.silu(z)
        y = y * jax.lax.rsqrt(jnp.mean(y * y, -1, keepdims=True) + 1e-06) * rms_w
        return x + y @ W_out

    def _L0_xattn_ref(Q, K, V, Wq, bq, Wk, bk, Wv, bv, Wo, bo):
        import jax, jax.numpy as jnp
        import numpy as np
        D_MODEL = 128
        NUM_HEAD = 16
        b, s, d = Q.shape
        h = NUM_HEAD
        hd = d // h
        q = (Q @ Wq.T + bq).reshape(b, s, h, hd)
        k = (K @ Wk.T + bk).reshape(b, s, h, hd)
        v = (V @ Wv.T + bv).reshape(b, s, h, hd)
        atten = jnp.einsum('bqhd,bkhd->bhqk', q, k) / jnp.sqrt(jnp.float32(hd))
        atten = jax.nn.softmax(atten, axis=3)
        out = jnp.einsum('bhqk,bkhv->bqhv', atten, v).reshape(b, s, d)
        return out @ Wo.T + bo

    def _L0_ffn_ref(inputs, gate_kernel, w0, w1, wo):
        import jax, jax.numpy as jnp
        import numpy as np
        E = 8
        TOPK = 2
        D = 128
        F = 512
        B, S = (2, 64)

        def _gmm(x, W, expert_onehot):
            return jnp.einsum('te,td,edf->tf', expert_onehot, x, W)
        dtype = inputs.dtype
        gate_logits = jnp.einsum('bsd,de->bse', inputs, gate_kernel)
        weights, selected_experts = jax.lax.top_k(gate_logits, TOPK)
        weights = jax.nn.softmax(weights.astype(jnp.float32), axis=-1).astype(dtype)
        inputs_2d = jnp.reshape(inputs, (-1, D))
        flat_sel = jnp.ravel(selected_experts)
        sort_idx = jnp.argsort(flat_sel)
        rep = jnp.repeat(inputs_2d, TOPK, axis=0)
        sorted_hidden = jnp.take(rep, sort_idx, axis=0)
        T = flat_sel.shape[0]
        group_sizes = jnp.zeros((E,), jnp.int32).at[flat_sel].add(1)
        expert_ids = jnp.repeat(jnp.arange(E), group_sizes, total_repeat_length=T)
        onehot = jax.nn.one_hot(expert_ids, E, dtype=dtype)
        layer_1 = _gmm(sorted_hidden, w0, onehot)
        layer_2 = _gmm(sorted_hidden, w1, onehot)
        intermediate = jax.nn.silu(layer_1) * layer_2
        layer_3 = _gmm(intermediate, wo, onehot)
        unsort = jnp.take(layer_3, jnp.argsort(sort_idx), axis=0)
        combined = unsort * jnp.ravel(weights)[:, None]
        out = jnp.sum(combined.reshape(-1, TOPK, D), axis=1)
        return out.reshape(inputs.shape).astype(dtype)
    x = _layernorm(x + _L0_attn_ref(x, L0_attn_ln_w, L0_attn_ln_b, L0_attn_W_in, L0_attn_dt_bias, L0_attn_A_log, L0_attn_D, L0_attn_rms_w, L0_attn_W_out), axis=-1)
    x = _layernorm(x + _L0_xattn_ref(x, ctx_1024, ctx_1024, L0_xattn_Wq, L0_xattn_bq, L0_xattn_Wk, L0_xattn_bk, L0_xattn_Wv, L0_xattn_bv, L0_xattn_Wo, L0_xattn_bo), axis=-1)
    x = _layernorm(x + _L0_ffn_ref(x, L0_ffn_gate_kernel, L0_ffn_w0, L0_ffn_w1, L0_ffn_wo), axis=-1)
    return x

_drawn_inputs = setup_inputs


def setup_inputs(seed=0):
    import zlib

    import numpy as np

    out = dict(_drawn_inputs(seed))
    spreads = {'L0_attn_ln_w': (1.0, 0.2),
     'L0_attn_ln_b': (0.0, 0.1),
     'L0_attn_rms_w': (1.0, 0.2),
     'L0_xattn_bq': (0.0, 0.8),
     'L0_xattn_bk': (0.0, 0.8),
     'L0_xattn_bv': (0.0, 0.1),
     'L0_xattn_bo': (0.0, 0.1)}
    factors = {'L0_attn_dt_bias': 4.858, 'L0_attn_A_log': 8.0, 'L0_xattn_Wq': 8.0, 'L0_xattn_Wk': 6.169}
    for name, (base, spread) in spreads.items():
        noise = np.random.default_rng([zlib.crc32(name.encode()), seed]).standard_normal(out[name].shape)
        drawn = base * np.exp(spread * noise) if base else spread * noise
        out[name] = jnp.asarray(drawn.astype(out[name].dtype))
    for name, factor in factors.items():
        out[name] = (out[name] * factor).astype(out[name].dtype)
    return out
```

```python
from contextlib import ExitStack

import numpy as np
import concourse.bass as bass
from concourse import mybir

F32 = mybir.dt.float32
F32R = mybir.dt.float32r
I32 = mybir.dt.int32
U32 = mybir.dt.uint32
ACT = mybir.ActivationFunctionType
ALU = mybir.AluOpType
AX_X = mybir.AxisListType.X

P = 128
B = 8
S = 256
D = 128
NT = B * S // P
TPS = S // P
DI = 256
NS = 32
NH = 4
HP = DI // NH
ROPE = NS // 2
DZ = 2 * DI + 2 * NS
DIN = DZ + NH
AH = 16
HD = D // AH
GJ = 4
GR = AH // GJ
NP = 4
NE = 8
FF = 512
FC = FF // P
BANK = 512


class Line:

    def __init__(self, eng, sem):
        self.eng, self.sem, self.n, self.seen = eng, sem, 0, {}

    def wait(self, *marks):
        for mark in marks:
            if mark is None:
                continue
            if isinstance(mark, list):
                self.wait(*mark)
                continue
            sem, value = mark
            if self.seen.get(id(sem), 0) < value:
                self.eng.wait_ge(sem, value)
                self.seen[id(sem)] = value

    def mark(self, ins):
        self.n += 1
        ins.then_inc(self.sem, 1)
        return self.sem, self.n


class Arrivals:

    def __init__(self, sem):
        self.sem, self.n = sem, 0

    def add(self, dma):
        self.n += 16
        dma.then_inc(self.sem, 16)
        return self.sem, self.n


def build(nc, A, out):
    ctx = ExitStack()
    with ctx:
        def sb(name, shape, dt=F32):
            return ctx.enter_context(nc.sbuf_tensor(name, shape, dt))

        def sem(name):
            return ctx.enter_context(nc.semaphore(name))

        psum = ctx.enter_context(nc.psum_tensor("banks", [P, 8, BANK], F32))

        def bank(n, k=1):
            return psum[:, n, :] if k == 1 else psum[:, n:n + k, :].rearrange("p k n -> p (k n)")

        pe = Line(nc.tensor, sem("s_pe"))
        dve = Line(nc.vector, sem("s_dve"))
        act = Line(nc.scalar, sem("s_act"))
        pool = Line(nc.gpsimd, sem("s_pool"))
        sp = Line(nc.sync, None)
        T, V, C, G = nc.tensor, nc.vector, nc.scalar, nc.gpsimd

        def arrivals(name):
            return Arrivals(sem(name))

        consts = sb("consts", [P, 3 * P])
        ident, causal, after = (consts[:, i * P:(i + 1) * P] for i in range(3))
        causal_r = sb("causal_r", [P, P], F32R)
        after_r = sb("after_r", [P, P], F32R)
        rope_cs = sb("rope_cs", [P, 2, TPS * 2 * ROPE])
        x_in = sb("x_in", [P, NT, D])
        x_twice = sb("x_twice", [P, NT, D])
        ctx_in = sb("ctx_in", [P, NT, D])
        w_in = sb("w_in", [P, DIN])
        w_out = sb("w_out", [P, 2, D])
        rms_w = sb("rms_w", [P, 2])
        ln_wb = sb("ln_wb", [P, 2])
        dt_bias = sb("dt_bias", [P, NH])
        neg_a = sb("neg_a", [P, NH])
        d_skip = sb("d_skip", [P, NH])
        wq, wk, wv, wo = (sb(n, [P, D]) for n in ("wq", "wk", "wv", "wo"))
        bqk = sb("bqk", [P, 2])
        bv, bo = sb("bv", [P, D]), sb("bo", [P, D])
        gate = sb("gate", [P, NE])
        stats = sb("stats", [P, NT, 6])
        mv = sb("mv", [P, NT, 2])
        rstd = sb("rstd", [P, NT])
        rs_u = sb("rs_u", [P, NT])
        rs_v = sb("rs_v", [P, NT])
        proj = sb("proj", [P, NT, DZ])
        dts = sb("dts", [P, NT, NH])
        sp_e = sb("sp_e", [P, NT * NH])
        sp_l = sb("sp_l", [P, NT * NH])
        sp_d = sb("sp_d", [P, NT * NH])
        sp_q = sb("sp_q", [P, NT * NH])
        a_raw = sb("a_raw", [P, NT, NH])
        a_hi = sb("a_hi", [P, NT, NH], F32R)
        a_lo = sb("a_lo", [P, NT, NH], F32R)
        ecs = sb("ecs", [P, NT, NH])
        dec = sb("dec", [P, NT, NH])
        rot = sb("rot", [P, NT * 2, NS])
        xn = sb("xn", [P, 2, D])
        hT = sb("hT", [P, 2, P])
        one = sb("one", [P, 1])
        keys = sb("keys", [P, B, GR, S], F32R)
        vals = sb("vals", [P, NT, AH, HD + 1])
        split_qk = sb("split_qk", [P, 2, 2, S], F32R)
        cT = sb("cT", [P, 2, S])
        x1 = sb("x1", [P, NT, D])

        q_dram = nc.dram_tensor("q_dram", [B, P, NP, S], F32, kind="Internal").ap()
        k_dram = nc.dram_tensor("k_dram", [B, P, NP, S], F32, kind="Internal").ap()

        a_x = [arrivals(f"a_x{g}") for g in range(4)]
        a_c = [arrivals(f"a_c{g}") for g in range(2)]
        a_w, a_w2 = arrivals("a_w"), arrivals("a_w2")

        def tiles(ap):
            return ap.rearrange("b (t p) d -> p (b t) d", p=P)

        def load(eng, group, dst, src):
            return group.add(eng.dma_start(dst, src))

        def rows(ap, n):
            return ap.unsqueeze(0).partition_broadcast(P).rearrange("a b n -> (a b) n") if False else \
                ap.rearrange("(o n) -> o n", o=1).to_broadcast([P, n])

        got_x = []
        for g in range(4):
            got_x.append(load(nc.sync, a_x[g], x_in[:, 4 * g:4 * g + 4, :], tiles(A["x"])[:, 4 * g:4 * g + 4, :]))
            if g == 0:
                load(nc.scalar, a_w, consts[:, :], A["consts"])
                load(nc.scalar, a_w, w_in[:, :], A["L0_attn_W_in"])
                load(nc.scalar, a_w, ln_wb[:, 0:1], A["L0_attn_ln_w"].rearrange("(p o) -> p o", o=1))
                load(nc.scalar, a_w, ln_wb[:, 1:2], A["L0_attn_ln_b"].rearrange("(p o) -> p o", o=1))
                got_w = load(nc.scalar, a_w, dt_bias[:, :], rows(A["L0_attn_dt_bias"], NH))
        got_c = [load(nc.sync, a_c[g], ctx_in[:, 8 * g:8 * g + 8, :], tiles(A["ctx_1024"])[:, 8 * g:8 * g + 8, :])
                 for g in range(2)]
        for dst, src in (
            (wk[:, :], A["wkT"]), (wv[:, :], A["wvT"]),
            (bqk[:, 0:1], A["L0_xattn_bq"].rearrange("(p o) -> p o", o=1)),
            (bqk[:, 1:2], A["L0_xattn_bk"].rearrange("(p o) -> p o", o=1)),
            (bv[:, :], rows(A["L0_xattn_bv"], D)), (bo[:, :], rows(A["L0_xattn_bo"], D)),
            (wq[:, :], A["wqT"]), (wo[:, :], A["woT"]),
            (rope_cs[:, :, :], A["rope"].rearrange("k p n -> p k n")),
            (w_out[:, :, :], A["L0_attn_W_out"].rearrange("(c p) n -> p c n", p=P)),
            (rms_w[:, :], A["rms_w2"]),
            (neg_a[:, :], rows(A["L0_attn_A_log"], NH)),
            (d_skip[:, :], rows(A["L0_attn_D"], NH)),
            (gate[:, :], A["L0_ffn_gate_kernel"]),
        ):
            got_w2 = load(nc.sync, a_w2, dst, src)

        m_one = dve.mark(V.memset(one[:, :], 1.0))

        def newton(y, v, u, w, steps, ready):
            m = ready
            for _ in range(steps):
                dve.wait(m)
                m = dve.mark(V.scalar_tensor_tensor(u, y, -0.5, y, ALU.mult, ALU.mult))
                dve.wait(m)
                m = dve.mark(V.tensor_tensor(w, u, v, ALU.mult))
                dve.wait(m)
                m = dve.mark(V.scalar_tensor_tensor(y, w, 1.5, y, ALU.add, ALU.mult))
            return m

        def rsqrt_bits(y, v, u, w, ready):
            dve.wait(ready)
            m = dve.mark(V.tensor_single_scalar(u.bitcast(I32), v.bitcast(I32), 1, ALU.arith_shift_right))
            dve.wait(m)
            m = dve.mark(V.tensor_scalar(y.bitcast(I32), u.bitcast(I32), -1.0, float(0x5F3759DF), ALU.mult, ALU.add))
            return newton(y, v, u, w, 4, m)

        def rsqrt_exp(y, v, eps, scale, u, w, ready):
            dve.wait(ready)
            m = dve.mark(V.tensor_scalar(v, v, scale, eps, ALU.mult, ALU.add))
            act.wait(m)
            m = act.mark(C.activation(u, v, ACT.Ln))
            act.wait(m)
            m = act.mark(C.activation(y, u, ACT.Exp, scale=-0.5))
            return newton(y, v, u, w, 1, m)

        C.preload_act_table_set("silu_and_others")
        normed = []
        for g in range(4):
            dve.wait(got_x[g])
            t0 = 4 * g
            m = [dve.mark(V.bn_stats(stats[:, t, :], x_in[:, t, :])) for t in range(t0, t0 + 4)]
            dve.wait(m[-1])
            m = [dve.mark(V.bn_aggr(mv[:, t, :], stats[:, t, :])) for t in range(t0, t0 + 4)]
            dve.wait(m[-1])
            var = mv[:, t0:t0 + 4, 1]
            m = dve.mark(V.tensor_scalar(rs_v[:, t0:t0 + 4], var, 1e-6, None, ALU.add))
            m = rsqrt_bits(rstd[:, t0:t0 + 4], rs_v[:, t0:t0 + 4], rs_u[:, t0:t0 + 4], mv[:, t0:t0 + 4, 1], m)
            normed.append(m)

        dve.wait(got_w)
        m_causal = dve.mark(V.tensor_copy(causal_r[:, :], causal))
        m_after = dve.mark(V.tensor_copy(after_r[:, :], after))

        zo = sb("zo", [P, 2, S])
        pool.mark(G.memset(zo[:, 0, :], 0.0))
        m_zo = pool.mark(G.memset(zo[:, 1, :], 1.0))
        a_init = arrivals("a_init")
        pool.wait(m_zo)
        for i, dram in enumerate((q_dram, k_dram)):
            for b in range(B):
                got_init = a_init.add(nc.gpsimd.dma_start(dram[b, :, 3, :], zo[:, i, :]))
        m_vals = pool.mark(G.memset(vals[:, :, :, HD:HD + 1], 1.0))

        freed_xn, freed_hT, freed_tp, freed_mm = [None] * 2, [None] * 2, [None] * 2, [None] * 2
        m_hT = [None] * NT
        m_proj = [None] * NT
        m_dts = [None] * NT
        for i in range(NT + 1):
            if i < NT:
                t, s = i, i % 2
                dve.wait(normed[t // 4], freed_xn[s])
                m = dve.mark(V.tensor_scalar(xn[:, s, :], x_in[:, t, :], mv[:, t, 0:1], rstd[:, t:t + 1],
                                             ALU.subtract, ALU.mult))
                pe.wait(got_w, m, freed_tp[s])
                m = freed_xn[s] = pe.mark(T.transpose(bank(s)[:, 0:P], xn[:, s, :], ident))
                act.wait(m, got_w, freed_hT[s])
                m_hT[t] = freed_tp[s] = act.mark(C.activation(hT[:, s, :], bank(s)[:, 0:P], ACT.Identity,
                                                              bias=ln_wb[:, 1:2], scale=ln_wb[:, 0:1]))
            if i >= 1:
                t, s = i - 1, (i - 1) % 2
                pb = bank(2 + 2 * s, 2)
                pe.wait(m_hT[t], *(freed_mm[s] or ()))
                pe.mark(T.matmul(pb[:, 0:BANK], hT[:, s, :], w_in[:, 0:BANK], start=True, stop=True))
                m = freed_hT[s] = pe.mark(T.matmul(pb[:, BANK:DIN], hT[:, s, :], w_in[:, BANK:DIN],
                                                   start=True, stop=True))
                act.wait(m)
                m_proj[t] = act.mark(C.activation(proj[:, t, :], pb[:, 0:DZ], ACT.Silu))
                dve.wait(m_proj[t])
                m_dts[t] = dve.mark(V.tensor_tensor(dts[:, t, :], pb[:, DZ:DIN], dt_bias[:, :], ALU.add))
                freed_mm[s] = (m_proj[t], m_dts[t])

        m_x2 = []
        freed_ctp = freed_kp = freed_vp = None
        freed_cT, freed_split = [None] * 2, [None] * 2
        a_kw, a_kr = [arrivals("a_kw0"), arrivals("a_kw1")], [arrivals(f"a_kr{b}") for b in range(B)]
        got_keys = [None] * B
        m_valsb = [None] * NT
        for b in range(B):
            s = b % 2
            pe.wait(got_c[b // 4], freed_ctp)
            for k in range(TPS):
                m = pe.mark(T.transpose(bank(6)[:, k * P:(k + 1) * P], ctx_in[:, TPS * b + k, :], ident))
            act.wait(m, freed_cT[s])
            m = freed_ctp = act.mark(C.activation(cT[:, s, :], bank(6)[:, 0:S], ACT.Identity))
            pe.wait(m, got_w2, freed_kp, freed_vp)
            m = pe.mark(T.matmul(bank(7)[:, 0:S], wk[:, :], cT[:, s, :], start=True, stop=True))
            for k in range(TPS):
                mv_ = pe.mark(T.matmul(bank(6)[:, S + k * P:S + (k + 1) * P], cT[:, s, k * P:(k + 1) * P], wv[:, :],
                                       start=True, stop=True))
            freed_cT[s] = mv_
            act.wait(m, freed_split[s])
            mk1 = act.mark(C.activation(split_qk[:, s, 0, :], bank(7)[:, 0:S], ACT.Identity, bias=bqk[:, 1:2]))
            dve.wait(mk1)
            mk2 = freed_kp = dve.mark(V.scalar_tensor_tensor(
                split_qk[:, s, 1, :], bank(7)[:, 0:S], bqk[:, 1:2], split_qk[:, s, 0, :].bitcast(F32),
                ALU.add, ALU.subtract))
            dve.wait(mv_, m_vals)
            for k in range(TPS):
                t = TPS * b + k
                m_valsb[t] = freed_vp = dve.mark(V.tensor_tensor(
                    vals[:, t, :, 0:HD], bank(6)[:, S + k * P:S + (k + 1) * P].rearrange("p (h d) -> p h d", d=HD),
                    bv[:, :].rearrange("p (h d) -> p h d", d=HD), ALU.add))
            freed_ctp = freed_vp
            sp.wait(mk1, mk2)
            head, rest = (split_qk[:, s, i, :].bitcast(F32) for i in range(2))
            a_kw[s].add(nc.sync.dma_start(k_dram[b, :, 0:3:2, :], head.unsqueeze(1).to_broadcast([P, 2, S])))
            freed_split[s] = a_kw[s].add(nc.sync.dma_start(k_dram[b, :, 1, :], rest))
            sp.wait(freed_split[s], got_init)
            for j in range(GJ):
                src = k_dram[b].rearrange("(j r d) c q -> j (d c) r q", j=GJ, r=GR)[j] if False else \
                    k_dram[b, 32 * j:32 * j + 32].rearrange("(r d) c q -> (d c) r q", r=GR)
                got_keys[b] = a_kr[b].add(nc.sync.dma_start(keys[32 * j:32 * j + 32, b, :, :].bitcast(F32), src))

        C.preload_act_table_set("natural_log_exp_and_others")
        flat = dts[:, :, :].rearrange("p t h -> p (t h)")
        dve.wait(m_dts[NT - 1])
        m = dve.mark(V.scalar_tensor_tensor(sp_d[:, :], flat, -1.0, flat, ALU.mult, ALU.min))
        act.wait(m, m_one)
        m_e = act.mark(C.activation(sp_e[:, :], sp_d[:, :], ACT.Exp))
        act.wait(m_e)
        m_l = act.mark(C.activation(sp_l[:, :], sp_e[:, :], ACT.Ln, bias=one[:, :]))
        dve.wait(m_e)
        m = dve.mark(V.tensor_scalar(sp_d[:, :], sp_e[:, :], 1.0, -1.0, ALU.add, ALU.add))
        dve.wait(m)
        m = dve.mark(V.tensor_single_scalar(sp_q[:, :], sp_d[:, :], 0.0, ALU.is_equal))
        dve.wait(m, m_l)
        dve.mark(V.tensor_tensor(sp_l[:, :], sp_l[:, :], sp_q[:, :], ALU.add))
        m = dve.mark(V.tensor_tensor(sp_d[:, :], sp_d[:, :], sp_q[:, :], ALU.add))
        dve.wait(m)
        m = dve.mark(V.reciprocal(sp_q[:, :], sp_d[:, :]))
        dve.wait(m)
        m = dve.mark(V.tensor_tensor(sp_l[:, :], sp_l[:, :], sp_q[:, :], ALU.mult))
        dve.wait(m)
        m = dve.mark(V.tensor_tensor(sp_l[:, :], sp_l[:, :], sp_e[:, :], ALU.mult))
        dve.wait(m)
        m_dt = dve.mark(V.scalar_tensor_tensor(flat, flat, 0.0, sp_l[:, :], ALU.max, ALU.add))
        act.wait(got_w2)
        m = act.mark(C.activation(neg_a[:, :], neg_a[:, :], ACT.Exp))
        dve.wait(m, m_dt)
        m = dve.mark(V.scalar_tensor_tensor(a_raw[:, :, :], dts[:, :, :], -1.0,
                                            neg_a[:, :].unsqueeze(1).to_broadcast([P, NT, NH]), ALU.mult, ALU.mult))
        dve.wait(m)
        m = dve.mark(V.tensor_copy(a_hi[:, :, :], a_raw[:, :, :]))
        dve.wait(m)
        m_a = dve.mark(V.tensor_tensor(a_lo[:, :, :], a_raw[:, :, :], a_hi[:, :, :].bitcast(F32), ALU.subtract))
        pe.wait(m_a, m_after, m_causal, *(m for f in freed_mm for m in f))
        for w, c0 in ((causal_r, 0), (after_r, NT * NH)):
            for part, a in enumerate((a_hi, a_lo)):
                m = pe.mark(T.matmul(bank(2)[:, c0:c0 + NT * NH], w[:, :], a[:, :, :].rearrange("p t h -> p (t h)"),
                                     start=part == 0, stop=part == 1))
        act.wait(m)
        act.mark(C.activation(ecs[:, :, :].rearrange("p t h -> p (t h)"), bank(2)[:, 0:NT * NH], ACT.Exp))
        m_dec = act.mark(C.activation(dec[:, :, :].rearrange("p t h -> p (t h)"),
                                      bank(2)[:, NT * NH:2 * NT * NH], ACT.Exp))
        bc = proj[:, :, 2 * DI:DZ].rearrange("p t (m n) -> p t m n", m=2)
        rsc = sb("rsc", [P, NT, 2, ROPE])
        rotv = rot[:, :, :].rearrange("p (t m) n -> p t m n", m=2)

        pool.wait(m_proj[NT - 1], got_w2)
        m_r = None
        for b in range(B):
            tt = slice(TPS * b, TPS * b + TPS)
            cosv, sinv = (rope_cs[:, i, :].rearrange("p (t m n) -> p t m n", t=TPS, m=2) for i in range(2))
            for e in range(2):
                for k in range(TPS):
                    m = pool.mark(G.tensor_tensor(rsc[:, TPS * b + k, :, e::2], bc[:, TPS * b + k, :, 1 - e:ROPE:2],
                                                  sinv[:, k, :, e::2], ALU.mult))
            for k in range(TPS):
                m2 = pool.mark(G.tensor_tensor(rotv[:, TPS * b + k, :, 0:ROPE], bc[:, TPS * b + k, :, 0:ROPE],
                                               cosv[:, k], ALU.mult))
            pool.wait(m2)
            pool.mark(G.tensor_tensor(rotv[:, tt, :, 0:ROPE], rotv[:, tt, :, 0:ROPE], rsc[:, tt], ALU.add))
            m_rot = pool.mark(G.tensor_copy(rotv[:, tt, :, ROPE:NS], bc[:, tt, :, ROPE:NS]))

        m_x2 = pool.mark(G.tensor_scalar(x_twice[:, :, :], x_in[:, :, :], 2.0, None, ALU.mult))
        for c in range(2):
            m_wo = pool.mark(G.tensor_scalar(w_out[:, c, :], w_out[:, c, :], rms_w[:, c:c + 1], None, ALU.mult))

        seg = sb("seg", [P, 2, 2, NH, P], F32R)
        decay = sb("decay", [P, 2, NH, P])
        bcT = sb("bcT", [NS, 2, 2, P])
        score = sb("score", [P, 2, P])
        xdt = sb("xdt", [P, 2, NH, HP])
        xdec = sb("xdec", [P, NH, HP])
        skip = sb("skip", [P, 2, NH, HP])
        state = sb("state", [NS, DI])
        y = sb("y", [P, 2, DI])
        ysq = sb("ysq", [P, DI])
        yoff = sb("yoff", [P, DI])
        ss = sb("ss", [P, 2, 4])
        yT = sb("yT", [P, 2, 2, P])
        r1 = sb("r1", [P, 2, D])
        st1 = sb("st1", [P, 2, 6])
        mv1 = sb("mv1", [P, 2, 2])
        nw = sb("nw", [P, 2, 4])

        W = {k: [None] * (NT + 8) for k in ("M", "scT", "xdt", "skip", "y", "rms", "x1", "bcT", "freeM", "freeBC",
                                           "freeY", "xdec", "Ddone", "exp", "freeyT", "state")}
        free = {}

        def mix_weights(t):
            s = t % 2
            pool.wait(m_a, m_causal, free.get(("seg", s)))
            dve.wait(m_a, m_causal, free.get(("seg", s)))
            m1 = dve.mark(V.tensor_tensor(
                seg[:, s, 0], causal.unsqueeze(1).to_broadcast([P, NH, P]),
                a_hi[:, t, :].bitcast(F32).unsqueeze(2).to_broadcast([P, NH, P]), ALU.mult))
            m2 = pool.mark(G.tensor_tensor(
                seg[:, s, 1], causal.unsqueeze(1).to_broadcast([P, NH, P]),
                a_lo[:, t, :].bitcast(F32).unsqueeze(2).to_broadcast([P, NH, P]), ALU.mult))
            pe.wait(m1, m2, free.get(("segbank", s)), m_dec)
            for part in range(2):
                m = pe.mark(T.matmul(bank(s), after_r[:, :], seg[:, s, part].rearrange("p h l -> p (h l)"),
                                     start=part == 0, stop=part == 1))
            free["seg", s] = m
            act.wait(m, free.get(("decay", s)))
            m_dec_t = free["segbank", s] = act.mark(C.activation(
                decay[:, s].rearrange("p h l -> p (h l)"), bank(s), ACT.Exp))
            pe.wait(m_rot, free.get("bcbank"))
            for i in range(2):
                m = pe.mark(T.transpose(bank(2)[0:NS, i * P:(i + 1) * P], rot[:, 2 * t + i, :], ident))
            act.wait(m, free.get(("bcT", s)))
            m_bcT = act.mark(C.activation(bcT[:, s].rearrange("p i l -> p (i l)"), bank(2)[0:NS, 0:2 * P],
                                          ACT.Identity))
            W["bcT"][t] = m_bcT
            pe.wait(m_bcT)
            m = pe.mark(T.matmul(bank(2)[:, 2 * P:3 * P], bcT[:, s, 0, :], bcT[:, s, 1, :], start=True, stop=True))
            dve.wait(m)
            m = free["bcbank"] = dve.mark(V.tensor_tensor(score[:, s, :], bank(2)[:, 2 * P:3 * P], causal, ALU.mult))
            dve.wait(m, m_dec_t)
            W["M"][t] = dve.mark(V.tensor_tensor(decay[:, s], decay[:, s],
                                                 score[:, s, :].unsqueeze(1).to_broadcast([P, NH, P]), ALU.mult))
            xs = proj[:, t, DI:2 * DI].rearrange("p (h c) -> p h c", h=NH)
            pool.wait(m_dt, free.get(("xdt", s)), free.get(("skip", s)))
            m = W["xdt"][t] = pool.mark(G.tensor_tensor(
                xdt[:, s], xs, dts[:, t, :].unsqueeze(2).to_broadcast([P, NH, HP]), ALU.mult))
            W["skip"][t] = pool.mark(G.tensor_tensor(
                skip[:, s], xs, d_skip[:, :].unsqueeze(2).to_broadcast([P, NH, HP]), ALU.mult))
            if t % TPS == 0:
                pool.wait(m, m_dec, free.get("xdec"))
                W["xdec"][t] = pool.mark(G.tensor_tensor(
                    xdec[:, :, :], xdt[:, s], dec[:, t, :].unsqueeze(2).to_broadcast([P, NH, HP]), ALU.mult))

        def mix(t):
            s = t % 2
            pe.wait(W["M"][t], W["xdt"][t], free.get("ybank"))
            for h in range(NH):
                m = pe.mark(T.matmul(bank(3)[:, h * HP:(h + 1) * HP], decay[:, s, h, :], xdt[:, s, h, :],
                                     start=True, stop=True))
            free["decay", s] = m
            free["xdt", s] = [m, W["xdec"][t]]
            if t % TPS == 0:
                pe.wait(W["xdec"][t], free.get("offbank"))
                m_st = pe.mark(T.matmul(bank(4)[0:NS, 0:DI], rot[:, 2 * t, :],
                                        xdec[:, :, :].rearrange("p h c -> p (h c)"), start=True, stop=True))
                free["xdec"] = m_st
                act.wait(m_st, free.get("state"))
                W["state"][t] = free["offbank"] = act.mark(C.activation(state[:, :], bank(4)[0:NS, 0:DI], ACT.Identity))
                free["bcT", s] = m
                add, m_add = skip[:, s].rearrange("p h c -> p (h c)"), W["skip"][t]
            else:
                pe.wait(W["state"][t - 1], free.get("offbank"))
                m_off = pe.mark(T.matmul(bank(4)[:, 0:DI], bcT[:, s, 1, :], state[:, :], start=True, stop=True))
                free["bcT", s] = free["state"] = m_off
                dve.wait(m_off, m_dec)
                m2 = free["offbank"] = dve.mark(V.tensor_tensor(
                    yoff[:, :].rearrange("p (h c) -> p h c", h=NH), bank(4)[:, 0:DI].rearrange("p (h c) -> p h c", h=NH),
                    ecs[:, t, :].unsqueeze(2).to_broadcast([P, NH, HP]), ALU.mult))
                dve.wait(m2, W["skip"][t])
                m_add = dve.mark(V.tensor_tensor(yoff[:, :], yoff[:, :], skip[:, s].rearrange("p h c -> p (h c)"), ALU.add))
                add = yoff[:, :]
            dve.wait(m, m_add, free.get(("y", s)))
            m = free["ybank"] = free["skip", s] = dve.mark(V.tensor_tensor(y[:, s, :], bank(3)[:, 0:DI], add, ALU.add))
            dve.wait(m)
            m = W["y"][t] = dve.mark(V.tensor_tensor(y[:, s, :], y[:, s, :], proj[:, t, 0:DI], ALU.mult))
            act.wait(m, free.get(("ss", s)))
            W["rms"][t] = act.mark(C.activation(ysq[:, :], y[:, s, :], ACT.Square, accum_out=ss[:, s, 0:1]))

        def mix_out(t):
            s = t % 2
            pe.wait(W["y"][t], free.get("yTbank"))
            for c in range(2):
                m = pe.mark(T.transpose(bank(5)[:, c * P:(c + 1) * P], y[:, s, c * P:(c + 1) * P], ident))
            free["y", s] = m
            act.wait(m, free.get(("yT", s)))
            m = free["yTbank"] = act.mark(C.activation(yT[:, s].rearrange("p c l -> p (c l)"), bank(5)[:, 0:DI],
                                                       ACT.Identity))
            pe.wait(m, m_wo, free.get("obank"))
            for c in range(2):
                m_o = pe.mark(T.matmul(bank(6)[:, 0:D], yT[:, s, c, :], w_out[:, c, :], start=c == 0, stop=c == 1))
            free["yT", s] = m_o
            m_rs = rsqrt_exp(ss[:, s, 1:2], ss[:, s, 0:1], 1e-6, 1.0 / DI, ss[:, s, 2:3], ss[:, s, 3:4],
                             W["rms"][t])
            dve.wait(m_rs, m_o, m_x2)
            m = free["obank"] = free["ss", s] = dve.mark(V.scalar_tensor_tensor(
                r1[:, s, :], bank(6)[:, 0:D], ss[:, s, 1:2], x_twice[:, t, :], ALU.mult, ALU.add))
            dve.wait(m)
            m = dve.mark(V.bn_stats(st1[:, s, :], r1[:, s, :]))
            dve.wait(m)
            m = dve.mark(V.bn_aggr(mv1[:, s, :], st1[:, s, :]))
            m = rsqrt_exp(nw[:, s, 0:1], mv1[:, s, 1:2], 1e-5, 1.0, nw[:, s, 1:2], nw[:, s, 2:3], m)
            dve.wait(m)
            W["x1"][t] = dve.mark(V.tensor_scalar(x1[:, t, :], r1[:, s, :], mv1[:, s, 0:1], nw[:, s, 0:1],
                                                  ALU.subtract, ALU.mult))

        a_qw, a_qr = [arrivals("a_qw0"), arrivals("a_qw1")], [arrivals(f"a_qr{i}") for i in range(2)]
        queries = sb("queries", [P, 2, GR, GJ, S], F32R)
        m_q0 = dve.mark(V.memset(queries[:, :, :, :, :].bitcast(F32), 0.0))
        x1T = sb("x1T", [P, S])
        got_q = [None] * B
        q_written = [None] * B

        def query(b):
            s = b % 2
            pe.wait(W["x1"][TPS * b + 1], free.get("qbank"), m_valsb[NT - 1])
            for k in range(TPS):
                m = pe.mark(T.transpose(bank(7)[:, k * P:(k + 1) * P], x1[:, TPS * b + k, :], ident))
            act.wait(m, free.get("x1T"))
            m = act.mark(C.activation(x1T[:, :], bank(7)[:, 0:S], ACT.Identity))
            pe.wait(m)
            m = free["x1T"] = pe.mark(T.matmul(bank(7)[:, S:2 * S], wq[:, :], x1T[:, :], start=True, stop=True))
            act.wait(m, freed_split[s])
            m1 = act.mark(C.activation(split_qk[:, s, 0, :], bank(7)[:, S:2 * S], ACT.Identity, bias=bqk[:, 0:1]))
            dve.wait(m1)
            m2 = free["qbank"] = dve.mark(V.scalar_tensor_tensor(
                split_qk[:, s, 1, :], bank(7)[:, S:2 * S], bqk[:, 0:1], split_qk[:, s, 0, :].bitcast(F32),
                ALU.add, ALU.subtract))
            sp.wait(m1, m2)
            head, rest = (split_qk[:, s, i, :].bitcast(F32) for i in range(2))
            a_qw[s].add(nc.sync.dma_start(q_dram[b, :, 0:2, :], head.unsqueeze(1).to_broadcast([P, 2, S])))
            q_written[b] = freed_split[s] = a_qw[s].add(nc.sync.dma_start(q_dram[b, :, 2, :], rest))

        for i in range(NT + 4):
            if i >= 4 and i % 2 == 1:
                query((i - 4) // 2)
            if 3 <= i < NT + 3 - 1 + 1:
                pass
            if 2 <= i < NT + 2:
                mix_out(i - 2)
            if 1 <= i < NT + 1:
                mix(i - 1)
            if i < NT:
                mix_weights(i)
        nm = sb("nm", [P, 2, TPS, AH])
        nm12 = sb("nm12", [AH, 2, 2, S], F32R)
        probs = ctx_in[:, :, :].rearrange("p t d -> p (t d)").rearrange("p (n i k q) -> p n i k q", n=2, i=2, k=TPS)
        a_mw, a_mr = [arrivals("a_mw0"), arrivals("a_mw1")], [arrivals("a_mr0"), arrivals("a_mr1")]
        SCALE = 1.0 / float(np.sqrt(np.float32(HD)))
        fq = [None, None]
        Am = {}

        def load_query(b):
            s = b % 2
            sp.wait(q_written[b], got_init, m_q0, fq[s])
            for j in range(GJ):
                src = q_dram[b, 32 * j:32 * j + 32].rearrange("(r d) c q -> (d c) r q", r=GR)
                got_q[b] = a_qr[s].add(nc.sync.dma_start(queries[32 * j:32 * j + 32, s, :, j, :].bitcast(F32), src))

        def maxima_unit(b, h, n):
            s, j, r, bk = b % 2, h // GR, h % GR, bank(n % 2)
            pe.wait(got_q[b], got_keys[b], free.get(("abank", n % 2)))
            for k in range(TPS):
                m = pe.mark(T.matmul(bk[:, k * S:(k + 1) * S], queries[:, s, r, j, k * P:(k + 1) * P],
                                     keys[:, b, r, :], start=True, stop=True))
            dve.wait(m)
            free["abank", n % 2] = Am[b] = dve.mark(V.tensor_reduce(
                nm[:, s, :, h], bk.rearrange("p (k q) -> p k q", k=TPS), AX_X, ALU.max, negate=True))

        def maxima_out(b):
            s = b % 2
            pe.wait(Am[b], free.get("misc"))
            for k in range(TPS):
                m = pe.mark(T.transpose(bank(7)[0:AH, k * P:(k + 1) * P], nm[:, s, k, :], ident))
            act.wait(m, free.get(("nm12", s)))
            m1 = act.mark(C.activation(nm12[:, s, 0, :], bank(7)[0:AH, 0:S], ACT.Identity))
            dve.wait(m1)
            m2 = free["misc"] = dve.mark(V.tensor_tensor(nm12[:, s, 1, :], bank(7)[0:AH, 0:S],
                                                         nm12[:, s, 0, :].bitcast(F32), ALU.subtract))
            sp.wait(m1, m2)
            dst = q_dram[b].rearrange("(h d) c q -> h d c q", d=HD)[:, 0:2, 3, :]
            m = free["nm12", s] = a_mw[s].add(nc.sync.dma_start(dst, nm12[:, s, :, :].bitcast(F32)))
            sp.wait(m, Am[b])
            for j in range(GJ):
                src = q_dram[b, 32 * j:32 * j + 32].rearrange("(r d) c q -> d c r q", r=GR)[0:2, 3]
                got_m = a_mr[s].add(nc.sync.dma_start(queries[32 * j + 3:32 * j + 8:4, s, :, j, :].bitcast(F32), src))
            return got_m

        def probs_unit(b, u, n, got_m):
            s, bk = b % 2, 2 + 2 * (n % 2)
            pe.wait(got_m, free.get(("bbank", n % 2)))
            for i in range(2):
                h = 2 * u + i
                j, r = h // GR, h % GR
                for k in range(TPS):
                    m = pe.mark(T.matmul(bank(bk + i)[:, k * S:(k + 1) * S], keys[:, b, r, k * P:(k + 1) * P],
                                         queries[:, s, r, j, :], start=True, stop=True))
            if u == AH // 2 - 1:
                fq[s] = m
            act.wait(m, free.get(("probs", n % 2)))
            m = free["bbank", n % 2] = act.mark(C.activation(
                probs[:, n % 2].rearrange("p i k q -> p (i k q)"), bank(bk, 2), ACT.Exp, scale=SCALE))
            return m

        def weigh_unit(b, u, n, m_exp):
            pe.wait(m_exp, m_valsb[NT - 1], free.get("avbank") if u == 0 else None)
            for i in range(2):
                h = 2 * u + i
                for q in range(TPS):
                    c0 = (q * AH + h) * (HD + 1)
                    for k in range(TPS):
                        m = pe.mark(T.matmul(bank(6)[:, c0:c0 + HD + 1], probs[:, n % 2, i, k, q * P:(q + 1) * P],
                                             vals[:, TPS * b + k, h, :], start=k == 0, stop=k == 1))
            free["probs", n % 2] = m
            return m

        x2 = x_in
        x2T = x_twice[:, :, :].rearrange("p t d -> p (t d)")
        rec = sb("rec", [P, TPS * AH])
        o_sb = sb("o_sb", [P, TPS, D])
        oT = hT[:, :, :].rearrange("p s l -> p (s l)")
        r2 = xn
        st2 = sb("st2", [P, TPS, 6])
        mv2 = sb("mv2", [P, TPS, 2])
        nw2 = sb("nw2", [P, 3, TPS])
        x1b = cT[:, :, :].rearrange("p s (k d) -> p s k d", k=TPS)
        m_x2 = [None] * B

        def attention_out(b, m_av):
            s = b % 2
            pool.wait(W["x1"][TPS * b + 1], free.get(("x1b", s)))
            m_xb = pool.mark(G.tensor_tensor(x1b[:, s], x1[:, TPS * b:TPS * b + TPS, :],
                                             bo[:, :].unsqueeze(1).to_broadcast([P, TPS, D]), ALU.add))
            av = bank(6)[:, 0:TPS * AH * (HD + 1)].rearrange("p (g c) -> p g c", c=HD + 1)
            dve.wait(m_av)
            m = dve.mark(V.reciprocal(rec[:, :], av[:, :, HD]))
            dve.wait(m, free.get("o_sb"))
            m = free["avbank"] = dve.mark(V.tensor_tensor(
                o_sb[:, :, :].rearrange("p k (h d) -> p (k h) d", d=HD), av[:, :, 0:HD],
                rec[:, :].unsqueeze(2).to_broadcast([P, TPS * AH, HD]), ALU.mult))
            pe.wait(m, free.get("misc"))
            for k in range(TPS):
                m = pe.mark(T.transpose(bank(7)[:, k * P:(k + 1) * P], o_sb[:, k, :], ident))
            free["o_sb"] = m
            act.wait(m, free.get("oT"))
            m = act.mark(C.activation(oT, bank(7)[:, 0:S], ACT.Identity))
            pe.wait(m)
            for k in range(TPS):
                m = pe.mark(T.matmul(bank(7)[:, S + k * P:S + (k + 1) * P], oT[:, k * P:(k + 1) * P], wo[:, :],
                                     start=True, stop=True))
            free["oT"] = m
            dve.wait(m, m_xb)
            m = free["x1b", s] = dve.mark(V.tensor_tensor(
                r2[:, :, :].rearrange("p k d -> p (k d)"), bank(7)[:, S:2 * S],
                x1b[:, s].rearrange("p k d -> p (k d)"), ALU.add))
            m_res = m
            dve.wait(m)
            m = [dve.mark(V.bn_stats(st2[:, k, :], r2[:, k, :])) for k in range(TPS)][-1]
            dve.wait(m)
            m = [dve.mark(V.bn_aggr(mv2[:, k, :], st2[:, k, :])) for k in range(TPS)][-1]
            m = rsqrt_exp(nw2[:, 0, :], mv2[:, :, 1], 1e-5, 1.0, nw2[:, 1, :], nw2[:, 2, :], m)
            dve.wait(m)
            for k in range(TPS):
                m = dve.mark(V.tensor_scalar(x2[:, TPS * b + k, :], r2[:, k, :], mv2[:, k, 0:1], nw2[:, 0, k:k + 1],
                                             ALU.subtract, ALU.mult))
            m_x2[b] = m
            pe.wait(m, m_res)
            for k in range(TPS):
                m = pe.mark(T.transpose(bank(7)[:, k * P:(k + 1) * P], x2[:, TPS * b + k, :], ident))
            act.wait(m)
            free["misc"] = act.mark(C.activation(x2T[:, b * S:(b + 1) * S], bank(7)[:, 0:S], ACT.Identity))
            return free["misc"]

        load_query(0)
        load_query(1)
        free["misc"] = free["qbank"]
        pe.wait(free["segbank", 0], free["segbank", 1], free["bcbank"], free["ybank"], free["offbank"],
                free["yTbank"], free["obank"])
        na = nb = 0
        for h in range(AH):
            maxima_unit(0, h, na)
            na += 1
        got_m = maxima_out(0)
        m_x2T = [None] * B
        for b in range(B):
            pending = None
            for u in range(AH // 2):
                m_exp = probs_unit(b, u, nb, got_m)
                if b + 1 < B:
                    for h in (2 * u, 2 * u + 1):
                        maxima_unit(b + 1, h, na)
                        na += 1
                if pending:
                    weigh_unit(b, *pending)
                pending = (u, nb, m_exp)
                nb += 1
            m_av = weigh_unit(b, *pending)
            if b + 1 < B:
                got_m = maxima_out(b + 1)
            if b + 2 < B:
                load_query(b + 2)
            m_x2T[b] = attention_out(b, m_av)

        build_moe(nc, A, out, locals())


def build_moe(nc, A, out, env):
    (sb, sem, bank, pe, dve, act, pool, sp, T, V, C, G, arrivals, free, proj, x2, x2T, gate, rsqrt_bits, m_x2T,
     consts) = (env[k] for k in "sb sem bank pe dve act pool sp T V C G arrivals free proj x2 x2T gate "
                "rsqrt_bits m_x2T consts".split())
    wts = proj[:, :, :].rearrange("p t n -> p (t n)")
    a_e = [arrivals("a_e0"), arrivals("a_e1")]
    EW = 3 * FF
    got_e = []
    sp.wait(free["ybank"], free["y", 0], free["y", 1], free["state"])
    free_e = [None, None]

    def load_expert(e):
        s = e % 2
        w = wts[:, s * EW:(s + 1) * EW]
        sp.wait(free_e[s])
        a_e[s].add(nc.sync.dma_start(w[:, 0:FF], A["L0_ffn_w0"][e]))
        a_e[s].add(nc.sync.dma_start(w[:, FF:2 * FF], A["L0_ffn_w1"][e]))
        got_e.append(a_e[s].add(nc.sync.dma_start(w[:, 2 * FF:].rearrange("p (c d) -> p c d", c=FC),
                                                  A["L0_ffn_wo"][e].rearrange("(c p) d -> p c d", p=P))))

    load_expert(0)
    load_expert(1)
    spare = env["rot"][:, :, :].rearrange("p t n -> p (t n)")

    def part(i, k):
        return spare[:, i * NT * NE:(i + k) * NT * NE]

    logit, top, topf, cw = (part(i, 1).rearrange("p (t e) -> p t e", e=NE) for i in range(4))
    oh = part(4, 2).rearrange("p (t k e) -> p t k e", k=2, e=NE)
    topi = sb("topi", [P, NT, 8], U32)
    wgt = sb("wgt", [P, NT, 2])
    iota = sb("iota", [P, NE])
    mi = [pool.mark(G.memset(iota[:, e:e + 1], float(e))) for e in range(NE)][-1]
    pe.wait(m_x2T[B - 1], *(free["abank", i] for i in range(2)))
    for t in range(NT):
        m = pe.mark(T.matmul(bank(0)[:, t * NE:(t + 1) * NE], x2T[:, t * P:(t + 1) * P], gate[:, :],
                             start=True, stop=True))
    dve.wait(m)
    m = dve.mark(V.tensor_copy(logit[:, :, :].rearrange("p t e -> p (t e)"), bank(0)[:, 0:NT * NE]))
    free_bank0 = m
    dve.wait(m)
    for t in range(NT):
        m = dve.mark(V.max(top[:, t, :], logit[:, t, :]))
    dve.wait(m)
    for t in range(NT):
        mI = dve.mark(V.max_index(topi[:, t, :], top[:, t, :], logit[:, t, :]))
    m = dve.mark(V.tensor_tensor(wgt[:, :, 1], top[:, :, 1], top[:, :, 0], ALU.subtract))
    act.wait(m)
    m = act.mark(C.activation(wgt[:, :, 1], wgt[:, :, 1], ACT.Exp))
    dve.wait(m)
    m = dve.mark(V.tensor_scalar(wgt[:, :, 0], wgt[:, :, 1], 1.0, None, ALU.add))
    dve.wait(m)
    m = dve.mark(V.reciprocal(wgt[:, :, 0], wgt[:, :, 0]))
    dve.wait(m)
    m = dve.mark(V.tensor_tensor(wgt[:, :, 1], wgt[:, :, 1], wgt[:, :, 0], ALU.mult))
    dve.wait(mI)
    m2 = dve.mark(V.tensor_copy(topf[:, :, :], topi[:, :, :]))
    dve.wait(m2, mi)
    for k in range(2):
        m2 = dve.mark(V.tensor_tensor(oh[:, :, k, :], iota[:, :].unsqueeze(1).to_broadcast([P, NT, NE]),
                                      topf[:, :, k].unsqueeze(2).to_broadcast([P, NT, NE]), ALU.is_equal))
    dve.wait(m, m2)
    for k in range(2):
        m = dve.mark(V.tensor_tensor(oh[:, :, k, :], oh[:, :, k, :],
                                     wgt[:, :, k].unsqueeze(2).to_broadcast([P, NT, NE]), ALU.mult))
    dve.wait(m)
    m_cw = dve.mark(V.tensor_tensor(cw[:, :, :], oh[:, :, 0, :], oh[:, :, 1, :], ALU.add))

    TB = 4 * P
    sil = wts[:, 2 * EW + 2 * FC * TB:2 * EW + (2 * FC + 2) * TB].rearrange("p (i t) -> p i t", i=2)
    hid = wts[:, 2 * EW:2 * EW + 2 * FC * TB].rearrange("p (i f t) -> p i f t", i=2, f=FC)
    m_hid = {}
    fr = {}
    acc = x2
    n = 0
    pe.wait(free_bank0, free["bbank", 0], free["bbank", 1], free["avbank"], free["misc"])
    dve.wait(m_x2T[B - 1])
    for e in range(NE):
        w = wts[:, (e % 2) * EW:(e % 2 + 1) * EW]
        for tb in range(NT // 4):
            xs = x2T[:, tb * TB:(tb + 1) * TB]
            hs = tb % 2
            for f in range(FC):
                i = n % 2
                pe.wait(got_e[e], fr.get(("g", i)))
                pe.mark(T.matmul(bank(2 * i), w[:, f * P:(f + 1) * P], xs, start=True, stop=True))
                m = pe.mark(T.matmul(bank(2 * i + 1), w[:, FF + f * P:FF + (f + 1) * P], xs, start=True, stop=True))
                act.wait(m, fr.get(("sil", i)))
                m = act.mark(C.activation(sil[:, i, :], bank(2 * i), ACT.Silu))
                dve.wait(m, fr.get(("hid", hs)))
                m = fr["g", i] = fr["sil", i] = dve.mark(V.tensor_tensor(hid[:, hs, f, :], bank(2 * i + 1), sil[:, i, :],
                                                                        ALU.mult))
                n += 1
            yb = bank(4 + tb % 2)
            pe.wait(m, fr.get(("y", tb % 2)))
            for k in range(4):
                for f in range(FC):
                    m = pe.mark(T.matmul(yb[:, k * P:(k + 1) * P], hid[:, hs, f, k * P:(k + 1) * P],
                                         w[:, 2 * FF + f * P:2 * FF + (f + 1) * P], start=f == 0, stop=f == FC - 1))
            fr["hid", hs] = m
            dve.wait(m, m_cw)
            for k in range(4):
                t = 4 * tb + k
                m2 = dve.mark(V.scalar_tensor_tensor(acc[:, t, :], yb[:, k * P:(k + 1) * P], cw[:, t, e:e + 1],
                                                     acc[:, t, :], ALU.mult, ALU.add))
            fr["y", tb % 2] = m2
            dve.wait(m2)
        free_e[e % 2] = m
        if e + 2 < NE:
            load_expert(e + 2)
    st, mv, r, u, v = env["stats"], env["mv"], env["rstd"], env["rs_u"], env["rs_v"]
    a_o = arrivals("a_o")
    ov = out.rearrange("b (t p) d -> p (b t) d", p=P)
    for g in range(4):
        sl = slice(4 * g, 4 * g + 4)
        m = [dve.mark(V.bn_stats(st[:, t, :], acc[:, t, :])) for t in range(4 * g, 4 * g + 4)][-1]
        dve.wait(m)
        m = [dve.mark(V.bn_aggr(mv[:, t, :], st[:, t, :])) for t in range(4 * g, 4 * g + 4)][-1]
        dve.wait(m)
        m = dve.mark(V.tensor_scalar(v[:, sl], mv[:, sl, 1], 1e-5, None, ALU.add))
        m = rsqrt_bits(r[:, sl], v[:, sl], u[:, sl], mv[:, sl, 1], m)
        dve.wait(m)
        for t in range(4 * g, 4 * g + 4):
            m = dve.mark(V.tensor_scalar(acc[:, t, :], acc[:, t, :], mv[:, t, 0:1], r[:, t:t + 1],
                                         ALU.subtract, ALU.mult))
        sp.wait(m)
        done = a_o.add(nc.sync.dma_start(ov[:, sl, :], acc[:, sl, :]))
    sp.wait(done)


def shape_constants():
    i = np.arange(P)
    consts = np.concatenate([np.eye(P), i[:, None] <= i[None, :], i[:, None] > i[None, :]], 1).astype(np.float32)
    inv = (1.0 / np.float32(10000.0) ** (np.arange(0, ROPE, 2, dtype=np.float32) / np.float32(ROPE))).astype(np.float32)
    ang = np.arange(S, dtype=np.float32)[:, None] * inv[None, :]
    cos, sin = np.cos(ang).astype(np.float32), np.sin(ang).astype(np.float32)
    cos = np.repeat(cos, 2, 1)
    sin = np.stack([-sin, sin], -1).reshape(S, ROPE)
    rope = np.stack([np.repeat(t.reshape(TPS, P, 1, ROPE), 2, 2).transpose(1, 0, 2, 3).reshape(P, -1) for t in (cos, sin)])
    return consts, np.ascontiguousarray(rope)


_INS = ["x", "ctx_1024", "L0_attn_ln_w", "L0_attn_ln_b", "L0_attn_W_in", "L0_attn_dt_bias", "L0_attn_A_log",
        "L0_attn_D", "L0_attn_W_out", "L0_xattn_bq", "L0_xattn_bk", "L0_xattn_bv", "L0_xattn_bo",
        "L0_ffn_gate_kernel", "L0_ffn_w0", "L0_ffn_w1", "L0_ffn_wo"]


def arrays_of(inputs):
    arrays = {n: np.ascontiguousarray(inputs[n]) for n in _INS}
    for n in "qkvo":
        arrays[f"w{n}T"] = np.ascontiguousarray(np.asarray(inputs[f"L0_xattn_W{n}"]).T)
    arrays["rms_w2"] = np.ascontiguousarray(np.asarray(inputs["L0_attn_rms_w"]).reshape(2, P).T)
    arrays["consts"], arrays["rope"] = shape_constants()
    return arrays


def kernel(**inputs):
    import concourse.bacc as bacc
    from concourse.bass_utils import run_bass_kernel_spmd

    nc = bacc.Bacc("TRN2", target_bir_lowering=False, num_devices=1)
    arrays = arrays_of(inputs)
    aps = {n: nc.dram_tensor(f"in_{n}", a.shape, F32, kind="ExternalInput").ap() for n, a in arrays.items()}
    out = nc.dram_tensor("out", (B, S, D), F32, kind="ExternalOutput").ap()
    build(nc, aps, out)
    r = run_bass_kernel_spmd(nc, [{f"in_{n}": a for n, a in arrays.items()}], core_ids=[0])
    return r.results[0]["out"]
```

```python
from contextlib import ExitStack

import numpy as np
import concourse.bass as bass
from concourse import mybir

F32 = mybir.dt.float32
F32R = mybir.dt.float32r
I32 = mybir.dt.int32
U32 = mybir.dt.uint32
ACT = mybir.ActivationFunctionType
ALU = mybir.AluOpType
AX_X = mybir.AxisListType.X

P = 128
B = 8
S = 256
D = 128
NT = B * S // P
TPS = S // P
DI = 256
NS = 32
NH = 4
HP = DI // NH
ROPE = NS // 2
DZ = 2 * DI + 2 * NS
DIN = DZ + NH
AH = 16
HD = D // AH
GJ = 4
GR = AH // GJ
NP = 4
NE = 8
FF = 512
FC = FF // P
BANK = 512


class Line:

    def __init__(self, eng, sem):
        self.eng, self.sem, self.n, self.seen = eng, sem, 0, {}

    def wait(self, *marks):
        for mark in marks:
            if mark is None:
                continue
            if isinstance(mark, list):
                self.wait(*mark)
                continue
            sem, value = mark
            if self.seen.get(id(sem), 0) < value:
                self.eng.wait_ge(sem, value)
                self.seen[id(sem)] = value

    def mark(self, ins):
        self.n += 1
        ins.then_inc(self.sem, 1)
        return self.sem, self.n


class Arrivals:

    def __init__(self, sem):
        self.sem, self.n = sem, 0

    def add(self, dma):
        self.n += 16
        dma.then_inc(self.sem, 16)
        return self.sem, self.n


def build(nc, A, out):
    ctx = ExitStack()
    with ctx:
        def sb(name, shape, dt=F32):
            return ctx.enter_context(nc.sbuf_tensor(name, shape, dt))

        def sem(name):
            return ctx.enter_context(nc.semaphore(name))

        psum = ctx.enter_context(nc.psum_tensor("banks", [P, 8, BANK], F32))

        def bank(n, k=1):
            return psum[:, n, :] if k == 1 else psum[:, n:n + k, :].rearrange("p k n -> p (k n)")

        pe = Line(nc.tensor, sem("s_pe"))
        dve = Line(nc.vector, sem("s_dve"))
        act = Line(nc.scalar, sem("s_act"))
        pool = Line(nc.gpsimd, sem("s_pool"))
        sp = Line(nc.sync, None)
        T, V, C, G = nc.tensor, nc.vector, nc.scalar, nc.gpsimd

        def arrivals(name):
            return Arrivals(sem(name))

        consts = sb("consts", [P, 3 * P])
        ident, causal, after = (consts[:, i * P:(i + 1) * P] for i in range(3))
        causal_r = sb("causal_r", [P, P], F32R)
        after_r = sb("after_r", [P, P], F32R)
        rope_cs = sb("rope_cs", [P, 2, TPS * 2 * ROPE])
        x_in = sb("x_in", [P, NT, D])
        x_twice = sb("x_twice", [P, NT, D])
        ctx_in = sb("ctx_in", [P, NT, D])
        w_in = sb("w_in", [P, DIN])
        w_out = sb("w_out", [P, 2, D])
        rms_w = sb("rms_w", [P, 2])
        ln_wb = sb("ln_wb", [P, 2])
        dt_bias = sb("dt_bias", [P, NH])
        neg_a = sb("neg_a", [P, NH])
        d_skip = sb("d_skip", [P, NH])
        wq, wk, wv, wo = (sb(n, [P, D]) for n in ("wq", "wk", "wv", "wo"))
        bqk = sb("bqk", [P, 2])
        bv, bo = sb("bv", [P, D]), sb("bo", [P, D])
        gate = sb("gate", [P, NE])
        stats = sb("stats", [P, NT, 6])
        mv = sb("mv", [P, NT, 2])
        rstd = sb("rstd", [P, NT])
        rs_u = sb("rs_u", [P, NT])
        rs_v = sb("rs_v", [P, NT])
        proj = sb("proj", [P, NT, DZ])
        dts = sb("dts", [P, NT, NH])
        sp_e = sb("sp_e", [P, NT * NH])
        sp_l = sb("sp_l", [P, NT * NH])
        sp_d = sb("sp_d", [P, NT * NH])
        sp_q = sb("sp_q", [P, NT * NH])
        a_raw = sb("a_raw", [P, NT, NH])
        a_hi = sb("a_hi", [P, NT, NH], F32R)
        a_lo = sb("a_lo", [P, NT, NH], F32R)
        ecs = sb("ecs", [P, NT, NH])
        dec = sb("dec", [P, NT, NH])
        rot = sb("rot", [P, NT * 2, NS])
        hT = sb("hT", [P, 2, P])
        one = sb("one", [P, 1])
        keys = sb("keys", [P, B, GR, S], F32R)
        vals = sb("vals", [P, NT, AH, HD + 1])
        split_qk = sb("split_qk", [P, 2, 2, S], F32R)
        cT = sb("cT", [P, 2, S])
        x1 = sb("x1", [P, NT, D])

        q_dram = nc.dram_tensor("q_dram", [B, P, NP, S], F32, kind="Internal").ap()
        k_dram = nc.dram_tensor("k_dram", [B, P, NP, S], F32, kind="Internal").ap()

        a_x = [arrivals(f"a_x{g}") for g in range(4)]
        a_c = [arrivals(f"a_c{g}") for g in range(2)]
        a_w, a_w2 = arrivals("a_w"), arrivals("a_w2")

        def tiles(ap):
            return ap.rearrange("b (t p) d -> p (b t) d", p=P)

        def load(eng, group, dst, src):
            return group.add(eng.dma_start(dst, src))

        def rows(ap, n):
            return ap.unsqueeze(0).partition_broadcast(P).rearrange("a b n -> (a b) n") if False else \
                ap.rearrange("(o n) -> o n", o=1).to_broadcast([P, n])

        got_x = []
        for g in range(4):
            got_x.append(load(nc.sync, a_x[g], x_in[:, 4 * g:4 * g + 4, :], tiles(A["x"])[:, 4 * g:4 * g + 4, :]))
            if g == 0:
                load(nc.scalar, a_w, consts[:, :], A["consts"])
                load(nc.scalar, a_w, w_in[:, :], A["L0_attn_W_in"])
                load(nc.scalar, a_w, ln_wb[:, 0:1], A["L0_attn_ln_w"].rearrange("(p o) -> p o", o=1))
                load(nc.scalar, a_w, ln_wb[:, 1:2], A["L0_attn_ln_b"].rearrange("(p o) -> p o", o=1))
                got_w = load(nc.scalar, a_w, dt_bias[:, :], rows(A["L0_attn_dt_bias"], NH))
        got_c = [load(nc.sync, a_c[g], ctx_in[:, 8 * g:8 * g + 8, :], tiles(A["ctx_1024"])[:, 8 * g:8 * g + 8, :])
                 for g in range(2)]
        for dst, src in (
            (wk[:, :], A["wkT"]), (wv[:, :], A["wvT"]),
            (bqk[:, 0:1], A["L0_xattn_bq"].rearrange("(p o) -> p o", o=1)),
            (bqk[:, 1:2], A["L0_xattn_bk"].rearrange("(p o) -> p o", o=1)),
            (bv[:, :], rows(A["L0_xattn_bv"], D)), (bo[:, :], rows(A["L0_xattn_bo"], D)),
            (wq[:, :], A["wqT"]), (wo[:, :], A["woT"]),
            (rope_cs[:, :, :], A["rope"].rearrange("k p n -> p k n")),
            (w_out[:, :, :], A["L0_attn_W_out"].rearrange("(c p) n -> p c n", p=P)),
            (rms_w[:, :], A["rms_w2"]),
            (neg_a[:, :], rows(A["L0_attn_A_log"], NH)),
            (d_skip[:, :], rows(A["L0_attn_D"], NH)),
            (gate[:, :], A["L0_ffn_gate_kernel"]),
        ):
            got_w2 = load(nc.sync, a_w2, dst, src)

        m_one = dve.mark(V.memset(one[:, :], 1.0))

        def newton(y, v, u, w, steps, ready, line=dve):
            m = ready
            for _ in range(steps):
                line.wait(m)
                m = line.mark(line.eng.tensor_tensor(u, y, y, ALU.mult))
                line.wait(m)
                m = line.mark(line.eng.tensor_tensor(w, u, v, ALU.mult))
                line.wait(m)
                m = line.mark(line.eng.tensor_scalar(u, w, -0.5, 1.5, ALU.mult, ALU.add))
                line.wait(m)
                m = line.mark(line.eng.tensor_tensor(y, y, u, ALU.mult))
            return m

        def rsqrt_bits(y, v, u, w, ready):
            dve.wait(ready)
            m = dve.mark(V.tensor_single_scalar(u.bitcast(I32), v.bitcast(I32), 1, ALU.arith_shift_right))
            dve.wait(m)
            m = dve.mark(V.tensor_scalar(y.bitcast(I32), u.bitcast(I32), -1.0, float(0x5F3759DF), ALU.mult, ALU.add))
            return newton(y, v, u, w, 3, m)

        def rsqrt_exp(y, v, eps, scale, u, w, ready, line=dve):
            line.wait(ready)
            m = line.mark(line.eng.tensor_scalar(v, v, scale, eps, ALU.mult, ALU.add))
            act.wait(m)
            m = act.mark(C.activation(u, v, ACT.Ln))
            act.wait(m)
            m = act.mark(C.activation(y, u, ACT.Exp, scale=-0.5))
            return newton(y, v, u, w, 1, m, line)

        C.preload_act_table_set("silu_and_others")
        xn = x1
        m_xn = [None] * NT

        def stats_group(t0, t1):
            m = []
            for t in range(t0, t1):
                dve.wait(got_x[t // 4])
                m.append(dve.mark(V.bn_stats(stats[:, t, :], x_in[:, t, :])))
            dve.wait(m[-1])
            m = [dve.mark(V.bn_aggr(mv[:, t, :], stats[:, t, :])) for t in range(t0, t1)]
            dve.wait(m[-1])
            m = dve.mark(V.tensor_scalar(rs_v[:, t0:t1], mv[:, t0:t1, 1], 1e-6, None, ALU.add))
            m = rsqrt_bits(rstd[:, t0:t1], rs_v[:, t0:t1], rs_u[:, t0:t1], mv[:, t0:t1, 1], m)
            dve.wait(m)
            for t in range(t0, t1):
                m_xn[t] = dve.mark(V.tensor_scalar(xn[:, t, :], x_in[:, t, :], mv[:, t, 0:1], rstd[:, t:t + 1],
                                                   ALU.subtract, ALU.mult))

        zo = sb("zo", [P, 2, S])
        pool.mark(G.memset(zo[:, 0, :], 0.0))
        m_zo = pool.mark(G.memset(zo[:, 1, :], 1.0))
        a_init = arrivals("a_init")
        pool.wait(m_zo)
        for i, dram in enumerate((k_dram, q_dram)):
            for b in range(B):
                got_init = a_init.add(nc.gpsimd.dma_start(dram[b, :, 3, :], zo[:, 1 - i, :]))
        m_vals = pool.mark(G.memset(vals[:, :, :, HD:HD + 1], 1.0))
        queries = sb("queries", [P, 2, GR, GJ, S], F32R)
        m_q0 = pool.mark(G.memset(queries[:, :, :, :, :].bitcast(F32), 0.0))
        pool.wait(*got_x)
        m_x2 = pool.mark(G.tensor_scalar(x_twice[:, :, :], x_in[:, :, :], 2.0, None, ALU.mult))

        stats_group(0, 4)
        dve.wait(got_w)
        m_causal = dve.mark(V.tensor_copy(causal_r[:, :], causal))
        m_after = dve.mark(V.tensor_copy(after_r[:, :], after))
        stats_group(4, NT)

        freed_hT, freed_tp, freed_mm = [None] * 2, [None] * 2, [None] * 2
        m_hT = [None] * NT
        m_proj = [None] * NT
        m_dts = [None] * NT
        freed_ctp = freed_kp = freed_vp = None
        freed_cT, freed_split = [None] * 2, [None] * 2
        a_kw, a_kr = [arrivals("a_kw0"), arrivals("a_kw1")], [arrivals(f"a_kr{b}") for b in range(B)]
        got_keys = [None] * B
        m_valsb = [None] * NT

        def turn_normed(t):
            s = t % 2
            pe.wait(got_w, m_xn[t], freed_tp[s])
            m = pe.mark(T.transpose(bank(s)[:, 0:P], xn[:, t, :], ident))
            act.wait(m, got_w, freed_hT[s])
            m_hT[t] = freed_tp[s] = act.mark(C.activation(hT[:, s, :], bank(s)[:, 0:P], ACT.Identity,
                                                          bias=ln_wb[:, 1:2], scale=ln_wb[:, 0:1]))

        def project(t):
            s = t % 2
            pb = bank(2 + 2 * s, 2)
            pe.wait(m_hT[t], freed_mm[s])
            pe.mark(T.matmul(pb[:, 0:BANK], hT[:, s, :], w_in[:, 0:BANK], start=True, stop=True))
            m = freed_hT[s] = pe.mark(T.matmul(pb[:, BANK:DIN], hT[:, s, :], w_in[:, BANK:DIN], start=True, stop=True))
            act.wait(m)
            m_proj[t] = act.mark(C.activation(proj[:, t, :], pb[:, 0:DZ], ACT.Silu))
            dve.wait(m_proj[t])
            m_dts[t] = dve.mark(V.tensor_tensor(dts[:, t, :], pb[:, DZ:DIN], dt_bias[:, :], ALU.add))
            freed_mm[s] = [m_proj[t], m_dts[t]]

        bc = proj[:, :, 2 * DI:DZ].rearrange("p t (m n) -> p t m n", m=2)
        rotv = rot[:, :, :].rearrange("p (t m) n -> p t m n", m=2)
        rsc = sb("rsc", [P, TPS, 2, ROPE])
        m_rot = [None] * B

        def rotate(b):
            tt = slice(TPS * b, TPS * b + TPS)
            cos, sin = (rope_cs[:, i, :].rearrange("p (t m n) -> p t m n", t=TPS, m=2) for i in range(2))
            dve.wait(m_proj[TPS * b + 1], got_w2)
            dve.wait(m_rot[b - 1])
            for e in range(2):
                dve.mark(V.tensor_tensor(rsc[:, :, :, e::2], bc[:, tt, :, 1 - e:ROPE:2], sin[:, :, :, e::2], ALU.mult))
            m = dve.mark(V.tensor_tensor(rotv[:, tt, :, 0:ROPE], bc[:, tt, :, 0:ROPE], cos, ALU.mult))
            dve.mark(V.tensor_copy(rotv[:, tt, :, ROPE:NS], bc[:, tt, :, ROPE:NS]))
            dve.wait(m)
            m_rot[b] = dve.mark(V.tensor_tensor(rotv[:, tt, :, 0:ROPE], rotv[:, tt, :, 0:ROPE], rsc[:, :, :, :], ALU.add))

        def turn_context(b):
            s = b % 2
            pe.wait(got_c[b // 4], fr_c["tp"])
            for k in range(TPS):
                m = pe.mark(T.transpose(bank(6)[:, k * P:(k + 1) * P], ctx_in[:, TPS * b + k, :], ident))
            act.wait(m, freed_cT[s])
            m_cT[b] = act.mark(C.activation(cT[:, s, :], bank(6)[:, 0:S], ACT.Identity))

        def keys_values(b):
            s = b % 2
            pe.wait(m_cT[b], got_w2, fr_c["kp"])
            m = pe.mark(T.matmul(bank(7)[:, 0:S], wk[:, :], cT[:, s, :], start=True, stop=True))
            for k in range(TPS):
                mv_ = pe.mark(T.matmul(bank(6)[:, S + k * P:S + (k + 1) * P], cT[:, s, k * P:(k + 1) * P], wv[:, :],
                                       start=True, stop=True))
            freed_cT[s] = mv_
            act.wait(m, freed_split[s])
            mk1 = act.mark(C.activation(split_qk[:, s, 0, :], bank(7)[:, 0:S], ACT.Identity, bias=bqk[:, 1:2]))
            dve.wait(mk1)
            mk2 = fr_c["kp"] = dve.mark(V.scalar_tensor_tensor(
                split_qk[:, s, 1, :], bank(7)[:, 0:S], bqk[:, 1:2], split_qk[:, s, 0, :].bitcast(F32),
                ALU.add, ALU.subtract))
            dve.wait(mv_, m_vals)
            for k in range(TPS):
                t = TPS * b + k
                m_valsb[t] = dve.mark(V.tensor_tensor(
                    vals[:, t, :, 0:HD], bank(6)[:, S + k * P:S + (k + 1) * P].rearrange("p (h d) -> p h d", d=HD),
                    bv[:, :].rearrange("p (h d) -> p h d", d=HD), ALU.add))
            fr_c["tp"] = m_valsb[t]
            sp.wait(mk1, mk2)
            head, rest = (split_qk[:, s, i, :].bitcast(F32) for i in range(2))
            a_kw[s].add(nc.sync.dma_start(k_dram[b, :, 0:3:2, :], head.unsqueeze(1).to_broadcast([P, 2, S])))
            freed_split[s] = a_kw[s].add(nc.sync.dma_start(k_dram[b, :, 1, :], rest))
            if b > 0:
                read_keys(b - 1)

        def read_keys(b):
            sp.wait(freed_split[b % 2], got_init)
            for j in range(GJ):
                src = k_dram[b, 32 * j:32 * j + 32].rearrange("(r d) c q -> (d c) r q", r=GR)
                got_keys[b] = a_kr[b].add(nc.sync.dma_start(keys[32 * j:32 * j + 32, b, :, :].bitcast(F32), src))

        fr_c, m_cT = {"tp": None, "kp": None}, [None] * B
        for i in range(NT + 1):
            if i < NT:
                turn_normed(i)
            if i >= 1:
                project(i - 1)
            if i % 2 == 1:
                turn_context(i // 2)
            elif i >= 2:
                keys_values(i // 2 - 1)
                rotate(i // 2 - 1)
        read_keys(B - 1)

        C.preload_act_table_set("natural_log_exp_and_others")
        flat = dts[:, :, :].rearrange("p t h -> p (t h)")
        dve.wait(m_dts[NT - 1])
        m = dve.mark(V.scalar_tensor_tensor(sp_d[:, :], flat, -1.0, flat, ALU.mult, ALU.min))
        act.wait(m, m_one)
        m_e = act.mark(C.activation(sp_e[:, :], sp_d[:, :], ACT.Exp))
        act.wait(m_e)
        m_l = act.mark(C.activation(sp_l[:, :], sp_e[:, :], ACT.Ln, bias=one[:, :]))
        dve.wait(m_e)
        m = dve.mark(V.tensor_scalar(sp_d[:, :], sp_e[:, :], 1.0, -1.0, ALU.add, ALU.add))
        dve.wait(m)
        m = dve.mark(V.tensor_single_scalar(sp_q[:, :], sp_d[:, :], 0.0, ALU.is_equal))
        dve.wait(m, m_l)
        dve.mark(V.tensor_tensor(sp_l[:, :], sp_l[:, :], sp_q[:, :], ALU.add))
        m = dve.mark(V.tensor_tensor(sp_d[:, :], sp_d[:, :], sp_q[:, :], ALU.add))
        dve.wait(m)
        m = dve.mark(V.reciprocal(sp_q[:, :], sp_d[:, :]))
        dve.wait(m)
        m = dve.mark(V.tensor_tensor(sp_l[:, :], sp_l[:, :], sp_q[:, :], ALU.mult))
        dve.wait(m)
        m = dve.mark(V.tensor_tensor(sp_l[:, :], sp_l[:, :], sp_e[:, :], ALU.mult))
        dve.wait(m)
        m_dt = dve.mark(V.scalar_tensor_tensor(flat, flat, 0.0, sp_l[:, :], ALU.max, ALU.add))
        act.wait(got_w2)
        m = act.mark(C.activation(neg_a[:, :], neg_a[:, :], ACT.Exp))
        dve.wait(m, m_dt)
        m = dve.mark(V.scalar_tensor_tensor(a_raw[:, :, :], dts[:, :, :], -1.0,
                                            neg_a[:, :].unsqueeze(1).to_broadcast([P, NT, NH]), ALU.mult, ALU.mult))
        dve.wait(m)
        m = dve.mark(V.tensor_copy(a_hi[:, :, :], a_raw[:, :, :]))
        dve.wait(m)
        m_a = dve.mark(V.tensor_tensor(a_lo[:, :, :], a_raw[:, :, :], a_hi[:, :, :].bitcast(F32), ALU.subtract))
        pe.wait(m_a, m_after, m_causal, *freed_mm)
        for w, c0 in ((causal_r, 0), (after_r, NT * NH)):
            for part, a in enumerate((a_hi, a_lo)):
                m = pe.mark(T.matmul(bank(2)[:, c0:c0 + NT * NH], w[:, :], a[:, :, :].rearrange("p t h -> p (t h)"),
                                     start=part == 0, stop=part == 1))
        act.wait(m)
        act.mark(C.activation(ecs[:, :, :].rearrange("p t h -> p (t h)"), bank(2)[:, 0:NT * NH], ACT.Exp))
        m_dec = act.mark(C.activation(dec[:, :, :].rearrange("p t h -> p (t h)"),
                                      bank(2)[:, NT * NH:2 * NT * NH], ACT.Exp))
        pool.wait(got_w2)
        for c in range(2):
            m_wo = pool.mark(G.tensor_scalar(w_out[:, c, :], w_out[:, c, :], rms_w[:, c:c + 1], None, ALU.mult))

        work = ctx_in[:, :, :].rearrange("p t d -> p (t d)")
        decay = work[:, 0:3 * NH * P].rearrange("p (r h l) -> p r h l", r=3, h=NH)
        score = work[:, 3 * NH * P:(3 * NH + 2) * P].rearrange("p (r l) -> p r l", r=2)
        seg = sb("seg", [P, 2, 2, NH, P], F32R)
        bcT = sb("bcT", [NS, 3, 2, P])
        xdt = sb("xdt", [P, 3, NH, HP])
        xdec = sb("xdec", [P, NH, HP])
        skip = sb("skip", [P, 3, NH, HP])
        state = sb("state", [NS, DI])
        y = sb("y", [P, 2, TPS, DI])
        ysq = sb("ysq", [P, DI])
        yoff = sb("yoff", [P, DI])
        ss = sb("ss", [P, 4, 2, TPS])
        yT = sb("yT", [P, TPS, 2, P])
        r1 = sb("r1", [P, 2, TPS, D])
        st1 = sb("st1", [P, TPS, 6])
        mv1 = sb("mv1", [P, 2, TPS, 2])
        nw = sb("nw", [P, 3, 2, TPS])
        x1T = sb("x1T", [P, S])

        free = {}
        m_bcT, m_dcy, m_xdt, m_skip, m_xdec, m_mat, m_y, m_sq = ({} for _ in range(8))

        def mix_exps(t):
            s, r = t % 2, t % 3
            for eng, part, a in ((dve, 0, a_hi), (pool, 1, a_lo)):
                eng.wait(m_a, m_causal, free.get(("seg", s)))
                m = eng.mark(eng.eng.tensor_tensor(
                    seg[:, s, part], causal.unsqueeze(1).to_broadcast([P, NH, P]),
                    a[:, t, :].bitcast(F32).unsqueeze(2).to_broadcast([P, NH, P]), ALU.mult))
                pe.wait(m)
            pe.wait(free.get(("segbank", s)), m_dec)
            for part in range(2):
                m = pe.mark(T.matmul(bank(s), after_r[:, :], seg[:, s, part].rearrange("p h l -> p (h l)"),
                                     start=part == 0, stop=part == 1))
            free["seg", s] = m
            act.wait(m, free.get(("decay", r)))
            m_dcy[t] = free["segbank", s] = act.mark(C.activation(decay[:, r].rearrange("p h l -> p (h l)"), bank(s), ACT.Exp))
            pe.wait(m_rot[t // TPS], free.get("bcbank"))
            for i in range(2):
                m = pe.mark(T.transpose(bank(2)[0:NS, i * P:(i + 1) * P], rot[:, 2 * t + i, :], ident))
            act.wait(m, free.get(("bcT", r)))
            m_bcT[t] = act.mark(C.activation(bcT[:, r].rearrange("p i l -> p (i l)"), bank(2)[0:NS, 0:2 * P], ACT.Identity))
            xs = proj[:, t, DI:2 * DI].rearrange("p (h c) -> p h c", h=NH)
            pool.wait(m_dt, free.get(("xdt", r)))
            m = m_xdt[t] = pool.mark(G.tensor_tensor(
                xdt[:, r], xs, dts[:, t, :].unsqueeze(2).to_broadcast([P, NH, HP]), ALU.mult))
            pool.wait(free.get(("skip", r)))
            m_skip[t] = pool.mark(G.tensor_tensor(
                skip[:, r], xs, d_skip[:, :].unsqueeze(2).to_broadcast([P, NH, HP]), ALU.mult))
            if t % TPS == 0:
                pool.wait(m, m_dec, free.get("xdec"))
                m_xdec[t] = pool.mark(G.tensor_tensor(
                    xdec[:, :, :], xdt[:, r], dec[:, t, :].unsqueeze(2).to_broadcast([P, NH, HP]), ALU.mult))

        def mix_matrix(t):
            s, r = t % 2, t % 3
            pe.wait(m_bcT[t])
            m = pe.mark(T.matmul(bank(2)[:, 2 * P:3 * P], bcT[:, r, 0, :], bcT[:, r, 1, :], start=True, stop=True))
            dve.wait(m)
            m = free["bcbank"] = dve.mark(V.tensor_tensor(score[:, s, :], bank(2)[:, 2 * P:3 * P], causal, ALU.mult))
            dve.wait(m, m_dcy[t])
            m_mat[t] = dve.mark(V.tensor_tensor(decay[:, r], decay[:, r],
                                                score[:, s, :].unsqueeze(1).to_broadcast([P, NH, P]), ALU.mult))

        def mix(t):
            k, r, bb = t % TPS, t % 3, (t // TPS) % 2
            if k == 0:
                pe.wait(m_xdec[t], free.get("offbank"))
                m_st = free["xdec"] = pe.mark(T.matmul(bank(4)[0:NS, 0:DI], rot[:, 2 * t, :],
                                                       xdec[:, :, :].rearrange("p h c -> p (h c)"), start=True, stop=True))
                act.wait(m_st, free.get("state"))
                m_state = free["offbank"] = act.mark(C.activation(state[:, :], bank(4)[0:NS, 0:DI], ACT.Identity))
                free["m_state"] = m_state
                add, m_add = skip[:, r].rearrange("p h c -> p (h c)"), m_skip[t]
            else:
                pe.wait(free["m_state"], free.get("offbank"))
                m_off = free["state"] = pe.mark(T.matmul(bank(4)[:, 0:DI], bcT[:, r, 1, :], state[:, :],
                                                         start=True, stop=True))
                dve.wait(m_off, m_dec)
                m2 = free["offbank"] = dve.mark(V.tensor_tensor(
                    yoff[:, :].rearrange("p (h c) -> p h c", h=NH), bank(4)[:, 0:DI].rearrange("p (h c) -> p h c", h=NH),
                    ecs[:, t, :].unsqueeze(2).to_broadcast([P, NH, HP]), ALU.mult))
                dve.wait(m2, m_skip[t])
                m_add = dve.mark(V.tensor_tensor(yoff[:, :], yoff[:, :], skip[:, r].rearrange("p h c -> p (h c)"), ALU.add))
                add = yoff[:, :]
            pe.wait(m_mat[t], m_xdt[t], free.get("ybank"))
            for h in range(NH):
                m = pe.mark(T.matmul(bank(3)[:, h * HP:(h + 1) * HP], decay[:, r, h, :], xdt[:, r, h, :],
                                     start=True, stop=True))
            free["decay", r] = free["bcT", r] = m
            free["xdt", r] = [m, m_xdec.get(t)]
            dve.wait(m, m_add, free.get(("y", bb)))
            m = free["ybank"] = free["skip", r] = dve.mark(V.tensor_tensor(y[:, bb, k, :], bank(3)[:, 0:DI], add, ALU.add))
            pool.wait(m)
            m = m_y[t] = pool.mark(G.tensor_tensor(y[:, bb, k, :], y[:, bb, k, :], proj[:, t, 0:DI], ALU.mult))
            act.wait(m, free.get(("ss", bb)), m_sq.get(t - 1))
            m_sq[t] = act.mark(C.activation(ysq[:, :], y[:, bb, k, :], ACT.Square, accum_out=ss[:, 0, bb, k:k + 1]))

        m_o, m_bn, m_rs1, m_x1, m_ln1 = ({} for _ in range(5))

        def mix_project(b):
            bb = b % 2
            pe.wait(m_y[TPS * b + 1], free.get("yTbank"))
            for k in range(TPS):
                for c in range(2):
                    m = pe.mark(T.transpose(bank(5)[:, (2 * k + c) * P:(2 * k + c + 1) * P],
                                            y[:, bb, k, c * P:(c + 1) * P], ident))
            free["y", bb] = [m, m_sq[TPS * b + 1]]
            act.wait(m, free.get("yT"))
            m = free["yTbank"] = act.mark(C.activation(yT[:, :, :, :].rearrange("p k c l -> p (k c l)"), bank(5), ACT.Identity))
            m_rs1[b] = rsqrt_exp(ss[:, 1, bb], ss[:, 0, bb], 1e-6, 1.0 / DI, ss[:, 2, bb], ss[:, 3, bb],
                                 m_sq[TPS * b + 1], pool)
            pe.wait(m, m_wo, free.get("obank"))
            for k in range(TPS):
                for c in range(2):
                    m = pe.mark(T.matmul(bank(6)[:, k * D:(k + 1) * D], yT[:, k, c, :], w_out[:, c, :],
                                         start=c == 0, stop=c == 1))
            free["yT"] = m_o[b] = m

        def mix_residual(b):
            bb = b % 2
            dve.wait(m_rs1[b], m_o[b], m_x2, free.get(("r1", bb)), free.get("st1"))
            for k in range(TPS):
                m = dve.mark(V.scalar_tensor_tensor(r1[:, bb, k, :], bank(6)[:, k * D:(k + 1) * D], ss[:, 1, bb, k:k + 1],
                                                    x_twice[:, TPS * b + k, :], ALU.mult, ALU.add))
            free["obank"] = free["ss", bb] = m
            dve.wait(m)
            m = [dve.mark(V.bn_stats(st1[:, k, :], r1[:, bb, k, :])) for k in range(TPS)][-1]
            dve.wait(m)
            m = [dve.mark(V.bn_aggr(mv1[:, bb, k, :], st1[:, k, :])) for k in range(TPS)][-1]
            m_ln1[b] = rsqrt_exp(nw[:, 0, bb], mv1[:, bb, :, 1], 1e-5, 1.0, nw[:, 1, bb], nw[:, 2, bb], m, pool)

        def mix_norm(b):
            bb = b % 2
            dve.wait(m_ln1[b])
            for k in range(TPS):
                m_x1[b] = free["r1", bb] = dve.mark(V.tensor_scalar(
                    x1[:, TPS * b + k, :], r1[:, bb, k, :], mv1[:, bb, k, 0:1], nw[:, 0, bb, k:k + 1],
                    ALU.subtract, ALU.mult))

        a_qw, a_qr = [arrivals("a_qw0"), arrivals("a_qw1")], [arrivals(f"a_qr{i}") for i in range(2)]
        got_q, q_written, m_x1T = [None] * B, [None] * B, {}

        def turn_x1(b):
            pe.wait(m_x1[b], free.get("qbank"), m_valsb[NT - 1])
            for k in range(TPS):
                m = pe.mark(T.transpose(bank(7)[:, k * P:(k + 1) * P], x1[:, TPS * b + k, :], ident))
            act.wait(m, free.get("x1T"))
            m_x1T[b] = act.mark(C.activation(x1T[:, :], bank(7)[:, 0:S], ACT.Identity))

        def query(b):
            s = b % 2
            pe.wait(m_x1T[b])
            m = free["x1T"] = pe.mark(T.matmul(bank(7)[:, S:2 * S], wq[:, :], x1T[:, :], start=True, stop=True))
            act.wait(m, freed_split[s])
            m1 = act.mark(C.activation(split_qk[:, s, 0, :], bank(7)[:, S:2 * S], ACT.Identity, bias=bqk[:, 0:1]))
            dve.wait(m1)
            m2 = free["qbank"] = dve.mark(V.scalar_tensor_tensor(
                split_qk[:, s, 1, :], bank(7)[:, S:2 * S], bqk[:, 0:1], split_qk[:, s, 0, :].bitcast(F32),
                ALU.add, ALU.subtract))
            sp.wait(m1, m2)
            head, rest = (split_qk[:, s, i, :].bitcast(F32) for i in range(2))
            a_qw[s].add(nc.sync.dma_start(q_dram[b, :, 0:2, :], head.unsqueeze(1).to_broadcast([P, 2, S])))
            q_written[b] = freed_split[s] = a_qw[s].add(nc.sync.dma_start(q_dram[b, :, 2, :], rest))

        for i in range(NT + 12):
            for stage, lag in ((query, 10), (turn_x1, 8), (mix_norm, 7), (mix_residual, 5), (mix_project, 4)):
                b, odd = divmod(i - lag, 2)
                if not odd and 0 <= b < B:
                    stage(b)
            for stage, lag in ((mix, 2), (mix_matrix, 1), (mix_exps, 0)):
                if 0 <= i - lag < NT:
                    stage(i - lag)

        nm = sb("nm", [P, 2, TPS, AH])
        nm12 = sb("nm12", [AH, 2, 2, S], F32R)
        probs = work.rearrange("p (n k q) -> p n k q", n=4, k=TPS)
        a_mw, a_mr = [arrivals("a_mw0"), arrivals("a_mw1")], [arrivals("a_mr0"), arrivals("a_mr1")]
        SCALE = 1.0 / float(np.sqrt(np.float32(HD)))
        freed_q = [None, None]
        m_max, got_max, m_x2d, m_x2T, m_av = {}, {}, [None] * B, [None] * B, {}
        MISC = bank(7)

        def load_query(b):
            s = b % 2
            sp.wait(q_written[b], got_init, m_q0, freed_q[s])
            for j in range(GJ):
                src = q_dram[b, 32 * j:32 * j + 32].rearrange("(r d) c q -> (d c) r q", r=GR)
                got_q[b] = a_qr[s].add(nc.sync.dma_start(queries[32 * j:32 * j + 32, s, :, j, :].bitcast(F32), src))

        def maxima(b, h, n):
            s, j, r, bk = b % 2, h // GR, h % GR, bank(n % 2)
            pe.wait(got_q[b], got_keys[b], free.get(("abank", n % 2)))
            for k in range(TPS):
                m = pe.mark(T.matmul(bk[:, k * S:(k + 1) * S], queries[:, s, r, j, k * P:(k + 1) * P],
                                     keys[:, b, r, :], start=True, stop=True))
            dve.wait(m, free.get(("nm", s)))
            free["abank", n % 2] = m_max[b] = dve.mark(V.tensor_reduce(
                nm[:, s, :, h], bk.rearrange("p (k q) -> p k q", k=TPS), AX_X, ALU.max, negate=True))

        def maxima_out(b):
            s = b % 2
            pe.wait(m_max[b], free.get("misc"))
            for k in range(TPS):
                m = free["nm", s] = pe.mark(T.transpose(MISC[0:AH, k * P:(k + 1) * P], nm[:, s, k, :], ident))
            act.wait(m, free.get(("nm12", s)))
            m1 = act.mark(C.activation(nm12[:, s, 0, :], MISC[0:AH, 0:S], ACT.Identity))
            dve.wait(m1)
            m2 = free["misc"] = dve.mark(V.tensor_tensor(nm12[:, s, 1, :], MISC[0:AH, 0:S],
                                                         nm12[:, s, 0, :].bitcast(F32), ALU.subtract))
            sp.wait(m1, m2)
            dst = q_dram[b].rearrange("(h d) c q -> h d c q", d=HD)[:, 0:2, 3, :]
            m = free["nm12", s] = a_mw[s].add(nc.sync.dma_start(dst, nm12[:, s, :, :].bitcast(F32)))
            sp.wait(m, m_max[b])
            for j in range(GJ):
                src = q_dram[b, 32 * j:32 * j + 32].rearrange("(r d) c q -> d c r q", r=GR)[0:2, 3]
                got_max[b] = a_mr[s].add(nc.sync.dma_start(
                    queries[32 * j + 3:32 * j + 8:4, s, :, j, :].bitcast(F32), src))

        m_exp = {}

        def exps(b, h):
            n = AH * b + h
            s, j, r, bk, e = b % 2, h // GR, h % GR, bank(2 + n % 3), n % 4
            pe.wait(got_max[b], free.get(("bbank", n % 3)))
            for k in range(TPS):
                m = pe.mark(T.matmul(bk[:, k * S:(k + 1) * S], keys[:, b, r, k * P:(k + 1) * P],
                                     queries[:, s, r, j, :], start=True, stop=True))
            if h == AH - 1:
                freed_q[s] = m
            act.wait(m, free.get(("probs", e)))
            m_exp[n] = free["bbank", n % 3] = act.mark(C.activation(
                probs[:, e].rearrange("p k q -> p (k q)"), bk, ACT.Exp, scale=SCALE))

        def weigh(n):
            b, h = divmod(n, AH)
            pe.wait(m_exp[n], free.get("avbank"))
            p0, c0 = 32 * (h % 4), (h // 4) * S
            for k in range(TPS):
                m = pe.mark(T.matmul(bank(5, 2)[p0:p0 + HD + 1, c0:c0 + S], vals[:, TPS * b + k, h, :],
                                     probs[:, n % 4, k, :], start=k == 0, stop=k == 1, tile_position=(0, p0)))
            free["probs", n % 4] = m
            m_av[b] = m

        avT = y[:, :, :, :].rearrange("p b k c -> p (b k c)")
        x2 = x_in
        x2T = x_twice[:, :, :].rearrange("p t d -> p (t d)")
        rec = sb("rec", [P, AH])
        o_sb = sb("o_sb", [P, TPS, D])
        oT = hT[:, :, :].rearrange("p s l -> p (s l)")
        r2 = w_in[:, 0:S].rearrange("p (k d) -> p k d", k=TPS)
        st2 = sb("st2", [P, TPS, 6])
        mv2 = sb("mv2", [P, TPS, 2])
        nw2 = sb("nw2", [P, 3, TPS])
        x1b = cT[:, 0, :].rearrange("p (k d) -> p k d", k=TPS)

        def attention_out(b):
            act.wait(m_av[b], free.get("avT"))
            m1 = act.mark(C.activation(avT[:, 0:BANK], bank(5), ACT.Identity))
            dve.wait(m_av[b], free.get("avT"))
            m2 = dve.mark(V.tensor_copy(avT[:, BANK:], bank(6)))
            free["avbank"] = [m1, m2]
            pool.wait(m_x1[b], free.get("x1b"))
            m_xb = pool.mark(G.tensor_tensor(x1b, x1[:, TPS * b:TPS * b + TPS, :],
                                             bo[:, :].unsqueeze(1).to_broadcast([P, TPS, D]), ALU.add))
            yield
            for q in range(TPS):
                pe.wait(m1, m2, free.get("misc"))
                for g in range(4):
                    m = pe.mark(T.transpose(MISC[:, g * P:(g + 1) * P], avT[:, g * S + q * P:g * S + (q + 1) * P], ident))
                free["avT"] = m
                av = MISC.rearrange("p (h c) -> p h c", c=32)
                dve.wait(m, free.get("rec"))
                m = dve.mark(V.reciprocal(rec[:, :], av[:, :, HD]))
                dve.wait(m, free.get("o_sb"))
                m_on = free["misc"] = free["rec"] = dve.mark(V.tensor_tensor(
                    o_sb[:, q, :].rearrange("p (h d) -> p h d", d=HD), av[:, :, 0:HD],
                    rec[:, :].unsqueeze(2).to_broadcast([P, AH, HD]), ALU.mult))
                yield
            pe.wait(m_on)
            for k in range(TPS):
                m = pe.mark(T.transpose(MISC[:, k * P:(k + 1) * P], o_sb[:, k, :], ident))
            free["o_sb"] = m
            act.wait(m, free.get("oT"))
            m_oT = free["misc"] = act.mark(C.activation(oT, MISC[:, 0:S], ACT.Identity))
            yield
            pe.wait(m_oT, free.get("misc"))
            for k in range(TPS):
                m = free["oT"] = pe.mark(T.matmul(MISC[:, k * P:(k + 1) * P], oT[:, k * P:(k + 1) * P], wo[:, :],
                                                  start=True, stop=True))
            dve.wait(m, m_xb, free.get("r2"))
            m = free["x1b"] = free["misc"] = dve.mark(V.tensor_tensor(
                r2.rearrange("p k d -> p (k d)"), MISC[:, 0:S], x1b.rearrange("p k d -> p (k d)"), ALU.add))
            dve.wait(m)
            m = [dve.mark(V.bn_stats(st2[:, k, :], r2[:, k, :])) for k in range(TPS)][-1]
            dve.wait(m)
            m = [dve.mark(V.bn_aggr(mv2[:, k, :], st2[:, k, :])) for k in range(TPS)][-1]
            yield
            m = rsqrt_exp(nw2[:, 0, :], mv2[:, :, 1], 1e-5, 1.0, nw2[:, 1, :], nw2[:, 2, :], m, pool)
            yield
            dve.wait(m, m_x2)
            for k in range(TPS):
                m = free["r2"] = dve.mark(V.tensor_scalar(
                    x2[:, TPS * b + k, :], r2[:, k, :], mv2[:, k, 0:1], nw2[:, 0, k:k + 1], ALU.subtract, ALU.mult))
            m_x2d[b] = m
            yield
            pe.wait(m, free.get("misc"))
            for k in range(TPS):
                m = pe.mark(T.transpose(MISC[:, k * P:(k + 1) * P], x2[:, TPS * b + k, :], ident))
            act.wait(m)
            m_x2T[b] = free["misc"] = act.mark(C.activation(x2T[:, b * S:(b + 1) * S], MISC[:, 0:S], ACT.Identity))
            yield

        load_query(0)
        load_query(1)
        free["misc"] = free["qbank"]
        mixer_done = [free[k] for k in (("segbank", 0), ("segbank", 1), "bcbank", "ybank", "offbank", "yTbank", "obank")]
        pe.wait(*mixer_done)
        dve.wait(*mixer_done)
        free["avbank"] = dve.mark(V.memset(bank(5, 2), 0.0))
        na = 0
        for h in range(AH):
            maxima(0, h, na)
            na += 1
        maxima_out(0)
        LAG = 2
        tail = iter(())
        for b in range(B):
            for h in range(AH):
                exps(b, h)
                if b + 1 < B and h < AH // 2:
                    for hh in (2 * h, 2 * h + 1):
                        maxima(b + 1, hh, na)
                        na += 1
                if AH * b + h >= LAG:
                    weigh(AH * b + h - LAG)
                if b and h == LAG - 1:
                    tail = attention_out(b - 1)
                if b + 1 < B and h == AH // 2:
                    maxima_out(b + 1)
                next(tail, None)
            for _ in tail:
                pass
            if b + 2 < B:
                load_query(b + 2)
        for n in range(AH * B - LAG, AH * B):
            weigh(n)
        for _ in attention_out(B - 1):
            pass

        build_moe(nc, A, out, locals())


def build_moe(nc, A, out, env):
    (sb, sem, bank, pe, dve, act, pool, sp, T, V, C, G, arrivals, free, proj, x2, x2T, gate, rsqrt_bits, m_x2T,
     consts) = (env[k] for k in "sb sem bank pe dve act pool sp T V C G arrivals free proj x2 x2T gate "
                "rsqrt_bits m_x2T consts".split())
    wts = proj[:, :, :].rearrange("p t n -> p (t n)")
    a_e = [arrivals("a_e0"), arrivals("a_e1")]
    EW = 3 * FF
    got_e = []
    sp.wait(free["y", 0], free["y", 1], free["ybank"])
    free_e = [None, None]

    def load_expert(e):
        s = e % 2
        w = wts[:, s * EW:(s + 1) * EW]
        sp.wait(free_e[s])
        a_e[s].add(nc.sync.dma_start(w[:, 0:FF], A["L0_ffn_w0"][e]))
        a_e[s].add(nc.sync.dma_start(w[:, FF:2 * FF], A["L0_ffn_w1"][e]))
        got_e.append(a_e[s].add(nc.sync.dma_start(w[:, 2 * FF:].rearrange("p (c d) -> p c d", c=FC),
                                                  A["L0_ffn_wo"][e].rearrange("(c p) d -> p c d", p=P))))

    load_expert(0)
    load_expert(1)
    spare = env["rot"][:, :, :].rearrange("p t n -> p (t n)")

    def part(i, k):
        return spare[:, i * NT * NE:(i + k) * NT * NE]

    logit, top, topf, cw = (part(i, 1).rearrange("p (t e) -> p t e", e=NE) for i in range(4))
    oh = part(4, 2).rearrange("p (t k e) -> p t k e", k=2, e=NE)
    topi = sb("topi", [P, NT, 8], U32)
    wgt = sb("wgt", [P, NT, 2])
    iota = sb("iota", [P, NE])
    mi = [pool.mark(G.memset(iota[:, e:e + 1], float(e))) for e in range(NE)][-1]
    pe.wait(m_x2T[B - 1], *(free["abank", i] for i in range(2)))
    for t in range(NT):
        m = pe.mark(T.matmul(bank(0)[:, t * NE:(t + 1) * NE], x2T[:, t * P:(t + 1) * P], gate[:, :],
                             start=True, stop=True))
    dve.wait(m)
    m = dve.mark(V.tensor_copy(logit[:, :, :].rearrange("p t e -> p (t e)"), bank(0)[:, 0:NT * NE]))
    free_bank0 = m
    dve.wait(m)
    for t in range(NT):
        m = dve.mark(V.max(top[:, t, :], logit[:, t, :]))
    dve.wait(m)
    for t in range(NT):
        mI = dve.mark(V.max_index(topi[:, t, :], top[:, t, :], logit[:, t, :]))
    m = dve.mark(V.tensor_tensor(wgt[:, :, 1], top[:, :, 1], top[:, :, 0], ALU.subtract))
    act.wait(m)
    m = act.mark(C.activation(wgt[:, :, 1], wgt[:, :, 1], ACT.Exp))
    dve.wait(m)
    m = dve.mark(V.tensor_scalar(wgt[:, :, 0], wgt[:, :, 1], 1.0, None, ALU.add))
    dve.wait(m)
    m = dve.mark(V.reciprocal(wgt[:, :, 0], wgt[:, :, 0]))
    dve.wait(m)
    m = dve.mark(V.tensor_tensor(wgt[:, :, 1], wgt[:, :, 1], wgt[:, :, 0], ALU.mult))
    dve.wait(mI)
    m2 = dve.mark(V.tensor_copy(topf[:, :, :], topi[:, :, :]))
    dve.wait(m2, mi)
    for k in range(2):
        m2 = dve.mark(V.tensor_tensor(oh[:, :, k, :], iota[:, :].unsqueeze(1).to_broadcast([P, NT, NE]),
                                      topf[:, :, k].unsqueeze(2).to_broadcast([P, NT, NE]), ALU.is_equal))
    dve.wait(m, m2)
    for k in range(2):
        m = dve.mark(V.tensor_tensor(oh[:, :, k, :], oh[:, :, k, :],
                                     wgt[:, :, k].unsqueeze(2).to_broadcast([P, NT, NE]), ALU.mult))
    dve.wait(m)
    m_cw = dve.mark(V.tensor_tensor(cw[:, :, :], oh[:, :, 0, :], oh[:, :, 1, :], ALU.add))

    TB = 4 * P
    sil = wts[:, 2 * EW + 2 * FC * TB:2 * EW + (2 * FC + 2) * TB].rearrange("p (i t) -> p i t", i=2)
    hid = wts[:, 2 * EW:2 * EW + 2 * FC * TB].rearrange("p (i f t) -> p i f t", i=2, f=FC)
    m_hid = {}
    fr = {}
    acc = x2
    n = 0
    pe.wait(free_bank0, *(free["bbank", i] for i in range(3)), free["avbank"], free["misc"])
    dve.wait(m_x2T[B - 1])
    for e in range(NE):
        w = wts[:, (e % 2) * EW:(e % 2 + 1) * EW]
        for tb in range(NT // 4):
            xs = x2T[:, tb * TB:(tb + 1) * TB]
            hs = tb % 2
            for f in range(FC):
                i = n % 2
                pe.wait(got_e[e], fr.get(("g", i)))
                pe.mark(T.matmul(bank(2 * i), w[:, f * P:(f + 1) * P], xs, start=True, stop=True))
                m = pe.mark(T.matmul(bank(2 * i + 1), w[:, FF + f * P:FF + (f + 1) * P], xs, start=True, stop=True))
                act.wait(m, fr.get(("sil", i)))
                m = act.mark(C.activation(sil[:, i, :], bank(2 * i), ACT.Silu))
                dve.wait(m, fr.get(("hid", hs)))
                m = fr["g", i] = fr["sil", i] = dve.mark(V.tensor_tensor(hid[:, hs, f, :], bank(2 * i + 1), sil[:, i, :],
                                                                        ALU.mult))
                n += 1
            yb = bank(4 + tb % 2)
            pe.wait(m, fr.get(("y", tb % 2)))
            for k in range(4):
                for f in range(FC):
                    m = pe.mark(T.matmul(yb[:, k * P:(k + 1) * P], hid[:, hs, f, k * P:(k + 1) * P],
                                         w[:, 2 * FF + f * P:2 * FF + (f + 1) * P], start=f == 0, stop=f == FC - 1))
            fr["hid", hs] = m
            dve.wait(m, m_cw)
            for k in range(4):
                t = 4 * tb + k
                m2 = dve.mark(V.scalar_tensor_tensor(acc[:, t, :], yb[:, k * P:(k + 1) * P], cw[:, t, e:e + 1],
                                                     acc[:, t, :], ALU.mult, ALU.add))
            fr["y", tb % 2] = m2
            dve.wait(m2)
        free_e[e % 2] = m
        if e + 2 < NE:
            load_expert(e + 2)
    st, mv, r, u, v = env["stats"], env["mv"], env["rstd"], env["rs_u"], env["rs_v"]
    a_o = arrivals("a_o")
    ov = out.rearrange("b (t p) d -> p (b t) d", p=P)
    for g in range(4):
        sl = slice(4 * g, 4 * g + 4)
        m = [dve.mark(V.bn_stats(st[:, t, :], acc[:, t, :])) for t in range(4 * g, 4 * g + 4)][-1]
        dve.wait(m)
        m = [dve.mark(V.bn_aggr(mv[:, t, :], st[:, t, :])) for t in range(4 * g, 4 * g + 4)][-1]
        dve.wait(m)
        m = dve.mark(V.tensor_scalar(v[:, sl], mv[:, sl, 1], 1e-5, None, ALU.add))
        m = rsqrt_bits(r[:, sl], v[:, sl], u[:, sl], mv[:, sl, 1], m)
        dve.wait(m)
        for t in range(4 * g, 4 * g + 4):
            m = dve.mark(V.tensor_scalar(acc[:, t, :], acc[:, t, :], mv[:, t, 0:1], r[:, t:t + 1],
                                         ALU.subtract, ALU.mult))
        sp.wait(m)
        done = a_o.add(nc.sync.dma_start(ov[:, sl, :], acc[:, sl, :]))
    sp.wait(done)


def shape_constants():
    i = np.arange(P)
    consts = np.concatenate([np.eye(P), i[:, None] <= i[None, :], i[:, None] > i[None, :]], 1).astype(np.float32)
    inv = (1.0 / np.float32(10000.0) ** (np.arange(0, ROPE, 2, dtype=np.float32) / np.float32(ROPE))).astype(np.float32)
    ang = np.arange(S, dtype=np.float32)[:, None] * inv[None, :]
    cos, sin = np.cos(ang).astype(np.float32), np.sin(ang).astype(np.float32)
    cos = np.repeat(cos, 2, 1)
    sin = np.stack([-sin, sin], -1).reshape(S, ROPE)
    rope = np.stack([np.repeat(t.reshape(TPS, P, 1, ROPE), 2, 2).transpose(1, 0, 2, 3).reshape(P, -1) for t in (cos, sin)])
    return consts, np.ascontiguousarray(rope)


_INS = ["x", "ctx_1024", "L0_attn_ln_w", "L0_attn_ln_b", "L0_attn_W_in", "L0_attn_dt_bias", "L0_attn_A_log",
        "L0_attn_D", "L0_attn_W_out", "L0_xattn_bq", "L0_xattn_bk", "L0_xattn_bv", "L0_xattn_bo",
        "L0_ffn_gate_kernel", "L0_ffn_w0", "L0_ffn_w1", "L0_ffn_wo"]


def arrays_of(inputs):
    arrays = {n: np.ascontiguousarray(inputs[n]) for n in _INS}
    for n in "qkvo":
        arrays[f"w{n}T"] = np.ascontiguousarray(np.asarray(inputs[f"L0_xattn_W{n}"]).T)
    arrays["rms_w2"] = np.ascontiguousarray(np.asarray(inputs["L0_attn_rms_w"]).reshape(2, P).T)
    arrays["consts"], arrays["rope"] = shape_constants()
    return arrays


def kernel(**inputs):
    import concourse.bacc as bacc
    from concourse.bass_utils import run_bass_kernel_spmd

    nc = bacc.Bacc("TRN2", target_bir_lowering=False, num_devices=1)
    arrays = arrays_of(inputs)
    aps = {n: nc.dram_tensor(f"in_{n}", a.shape, F32, kind="ExternalInput").ap() for n, a in arrays.items()}
    out = nc.dram_tensor("out", (B, S, D), F32, kind="ExternalOutput").ap()
    build(nc, aps, out)
    r = run_bass_kernel_spmd(nc, [{f"in_{n}": a for n, a in arrays.items()}], core_ids=[0])
    return r.results[0]["out"]
```

```python
from contextlib import ExitStack

import numpy as np
import concourse.bass as bass
from concourse import mybir

F32 = mybir.dt.float32
F32R = mybir.dt.float32r
I32 = mybir.dt.int32
U32 = mybir.dt.uint32
BF16 = mybir.dt.bfloat16
ACT = mybir.ActivationFunctionType
ALU = mybir.AluOpType
AX_X = mybir.AxisListType.X

P = 128
B = 8
S = 256
D = 128
NT = B * S // P
TPS = S // P
DI = 256
NS = 32
NH = 4
HP = DI // NH
ROPE = NS // 2
DZ = 2 * DI + 2 * NS
DIN = DZ + NH
AH = 16
HD = D // AH
GJ = 4
GR = AH // GJ
KR = 3
NP = 4
NE = 8
FF = 512
FC = FF // P
BANK = 512
TOPK = 2
T = B * S
SLOT_TILES = TOPK * T // P + NE - 1
LT = T // P
PAIRS = T * TOPK
W_HEAD, W_REST, W_OUT, W_ALL = 0, 2 * FF, 4 * FF, 6 * FF


class Line:

    def __init__(self, eng, sem):
        self.eng, self.sem, self.n, self.seen = eng, sem, 0, {}

    def wait(self, *marks):
        for mark in marks:
            if mark is None:
                continue
            if isinstance(mark, list):
                self.wait(*mark)
                continue
            sem, value = mark
            if self.seen.get(id(sem), 0) < value:
                self.eng.wait_ge(sem, value)
                self.seen[id(sem)] = value

    def mark(self, ins):
        self.n += 1
        ins.then_inc(self.sem, 1)
        return self.sem, self.n


class Arrivals:

    def __init__(self, sem):
        self.sem, self.n = sem, 0

    def add(self, dma):
        self.n += 16
        dma.then_inc(self.sem, 16)
        return self.sem, self.n


def build(nc, A, out):
    ctx = ExitStack()
    with ctx:
        def sb(name, shape, dt=F32):
            return ctx.enter_context(nc.sbuf_tensor(name, shape, dt))

        def sem(name):
            return ctx.enter_context(nc.semaphore(name))

        psum = ctx.enter_context(nc.psum_tensor("banks", [P, 8, BANK], F32))

        def bank(n, k=1):
            return psum[:, n, :] if k == 1 else psum[:, n:n + k, :].rearrange("p k n -> p (k n)")

        pe = Line(nc.tensor, sem("s_pe"))
        dve = Line(nc.vector, sem("s_dve"))
        act = Line(nc.scalar, sem("s_act"))
        pool = Line(nc.gpsimd, sem("s_pool"))
        sp = Line(nc.sync, None)
        TE, V, C, G = nc.tensor, nc.vector, nc.scalar, nc.gpsimd

        def arrivals(name):
            return Arrivals(sem(name))

        consts = sb("consts", [P, 6 * P + 2])
        ident, causal, after, before, iota, expert_offset = (consts[:, i * P:(i + 1) * P] for i in range(6))
        token_no, spare_row = (consts[:, 6 * P + i:6 * P + i + 1] for i in range(2))
        x_in = sb("x_in", [P, NT, D])
        x_twice = sb("x_twice", [P, NT, D])
        ctx_in = sb("ctx_in", [P, NT, D])
        w_in = sb("w_in", [P, DIN])
        rms_w = sb("rms_w", [P, 2])
        ln_wb = sb("ln_wb", [P, 2])
        dt_bias = sb("dt_bias", [P, NH])
        d_skip = sb("d_skip", [P, NH])
        wq, wk, wv, wo = (sb(n, [P, D]) for n in ("wq", "wk", "wv", "wo"))
        bqk = sb("bqk", [P, 2])
        bv, bo = sb("bv", [P, D]), sb("bo", [P, D])
        gate = sb("gate", [P, NE])
        stats = sb("stats", [P, NT, 6])
        mv = sb("mv", [P, NT, 2])
        rstd = sb("rstd", [P, NT])
        rs_u = sb("rs_u", [P, NT])
        rs_v = sb("rs_v", [P, NT])
        one = sb("one", [P, 1])
        keys = sb("keys", [P, KR, GR, S], F32R)
        vals = sb("vals", [P, NT, AH, HD + 1])
        cT = sb("cT", [P, 2, S])
        x1 = sb("x1", [P, NT, D])

        queries = sb("queries", [P, 2, GR, GJ, S], F32R)
        y = sb("y", [P, 2, TPS, DI])
        nm = sb("nm", [P, 2, TPS, AH])
        nm12 = sb("nm12", [AH, 2, S], F32R)
        rec = sb("rec", [P, AH])
        o_sb = sb("o_sb", [P, TPS, D])
        st2 = sb("st2", [P, TPS, 6])
        mv2 = sb("mv2", [P, TPS, 2])
        nw2 = sb("nw2", [P, 3, TPS])
        logit = sb("logit", [P, TPS, NE])
        top = sb("top", [P, TPS, 8])
        topi = sb("topi", [P, TPS, 8], U32)
        topf = sb("topf", [P, TPS, 8])
        wgt = sb("wgt", [P, NT, TOPK])
        choice = sb("choice", [P, TOPK, TPS, NE])
        chosen = sb("chosen", [P, TPS, NE], BF16)
        before_b = sb("before_b", [P, P], BF16)
        ones_b = sb("ones_b", [P, P], BF16)
        ident_r = sb("ident_r", [P, P], F32R)
        count = sb("count", [P, NE])
        rank = sb("rank", [P, TPS, NE])
        picked = sb("picked", [P, TOPK, TPS, NE])
        place = sb("place", [P, TOPK * TPS])
        place_i = sb("place_i", [P, TOPK * TPS], I32)
        part_i = sb("part_i", [P, 2, TOPK * TPS], I32)
        part_f = sb("part_f", [P, 2, TOPK * TPS])
        column = sb("column", [P, TOPK * TPS])
        row_hot = sb("row_hot", [P, TOPK * TPS, P], BF16)
        col_hot = sb("col_hot", [P, TOPK * TPS, 2, P], BF16)
        table = sb("table", [P, P])
        x2_split = sb("x2_split", [P, TPS, 2, D], F32R)

        mixer = ExitStack()

        def msb(name, shape, dt=F32):
            return mixer.enter_context(nc.sbuf_tensor(name, shape, dt))

        causal_r = msb("causal_r", [P, P], F32R)
        after_r = msb("after_r", [P, P], F32R)
        rope_cs = msb("rope_cs", [P, 2, TPS * 2 * ROPE])
        hT = msb("hT", [P, 2, P])
        w_out = msb("w_out", [P, 2, D])
        neg_a = msb("neg_a", [P, NH])
        proj = msb("proj", [P, NT, DZ])
        dts = msb("dts", [P, NT, NH])
        sp_e = msb("sp_e", [P, NT * NH])
        sp_l = msb("sp_l", [P, NT * NH])
        sp_d = msb("sp_d", [P, NT * NH])
        sp_q = msb("sp_q", [P, NT * NH])
        a_raw = msb("a_raw", [P, NT, NH])
        a_hi = msb("a_hi", [P, NT, NH], F32R)
        a_lo = msb("a_lo", [P, NT, NH], F32R)
        ecs = msb("ecs", [P, NT, NH])
        dec = msb("dec", [P, NT, NH])
        rot = msb("rot", [P, NT * 2, NS])
        split_qk = msb("split_qk", [P, 2, 2, S], F32R)
        rsc = msb("rsc", [P, TPS, 2, ROPE])
        seg = msb("seg", [P, 3, 2, NH, P], F32R)
        bcT = msb("bcT", [NS, 3, 2, P])
        xdt = msb("xdt", [P, 4, NH, HP])
        xdec = msb("xdec", [P, 2, NH, HP])
        skip = msb("skip", [P, 4, NH, HP])
        state = msb("state", [NS, DI])
        ysq = msb("ysq", [P, DI])
        yoff = msb("yoff", [P, DI])
        ss = msb("ss", [P, 4, 2, TPS])
        r1 = msb("r1", [P, 2, TPS, D])
        st1 = msb("st1", [P, TPS, 6])
        mv1 = msb("mv1", [P, 2, TPS, 2])
        nw = msb("nw", [P, 3, 2, TPS])

        q_dram = nc.dram_tensor("q_dram", [B, P, NP, S], F32, kind="Internal").ap()
        k_dram = nc.dram_tensor("k_dram", [B, P, NP, S], F32, kind="Internal").ap()
        x2_dram = nc.dram_tensor("x2_dram", [T, 2 * D], F32, kind="Internal").ap()
        y_dram = nc.dram_tensor("y_dram", [PAIRS + P, D], F32, kind="Internal").ap()

        a_x = [arrivals(f"a_x{g}") for g in range(4)]
        a_c = [arrivals(f"a_c{g}") for g in range(2)]
        a_w, a_w2 = arrivals("a_w"), arrivals("a_w2")

        def tiles(ap):
            return ap.rearrange("b (t p) d -> p (b t) d", p=P)

        def load(eng, group, dst, src):
            return group.add(eng.dma_start(dst, src))

        def rows(ap, n):
            return ap.rearrange("(o n) -> o n", o=1).to_broadcast([P, n])

        got_x = []
        for g in range(4):
            got_x.append(load(nc.sync, a_x[g], x_in[:, 4 * g:4 * g + 4, :], tiles(A["x"])[:, 4 * g:4 * g + 4, :]))
            if g == 0:
                load(nc.scalar, a_w, consts[:, 0:3 * P], A["consts"][:, 0:3 * P])
                load(nc.scalar, a_w, w_in[:, :], A["L0_attn_W_in"])
                load(nc.scalar, a_w, ln_wb[:, 0:1], A["L0_attn_ln_w"].rearrange("(p o) -> p o", o=1))
                load(nc.scalar, a_w, ln_wb[:, 1:2], A["L0_attn_ln_b"].rearrange("(p o) -> p o", o=1))
                got_w = load(nc.scalar, a_w, dt_bias[:, :], rows(A["L0_attn_dt_bias"], NH))
        got_c = [load(nc.sync, a_c[g], ctx_in[:, 8 * g:8 * g + 8, :], tiles(A["ctx_1024"])[:, 8 * g:8 * g + 8, :])
                 for g in range(2)]
        for dst, src in (
            (consts[:, 3 * P:], A["consts"][:, 3 * P:]), (wk[:, :], A["wkT"]), (wv[:, :], A["wvT"]),
            (bqk[:, 0:1], A["L0_xattn_bq"].rearrange("(p o) -> p o", o=1)),
            (bqk[:, 1:2], A["L0_xattn_bk"].rearrange("(p o) -> p o", o=1)),
            (bv[:, :], rows(A["L0_xattn_bv"], D)), (bo[:, :], rows(A["L0_xattn_bo"], D)),
            (wq[:, :], A["wqT"]), (wo[:, :], A["woT"]),
            (rope_cs[:, :, :], A["rope"].rearrange("k p n -> p k n")),
            (w_out[:, :, :], A["L0_attn_W_out"].rearrange("(c p) n -> p c n", p=P)),
            (rms_w[:, :], A["rms_w2"]),
            (neg_a[:, :], rows(A["L0_attn_A_log"], NH)),
            (d_skip[:, :], rows(A["L0_attn_D"], NH)),
            (gate[:, :], A["L0_ffn_gate_kernel"]),
        ):
            got_w2 = load(nc.sync, a_w2, dst, src)

        m_one = dve.mark(V.memset(one[:, :], 1.0))

        def newton(y, v, u, w, steps, ready, line=dve):
            m = ready
            for _ in range(steps):
                line.wait(m)
                m = line.mark(line.eng.tensor_tensor(u, y, y, ALU.mult))
                line.wait(m)
                m = line.mark(line.eng.tensor_tensor(w, u, v, ALU.mult))
                line.wait(m)
                m = line.mark(line.eng.tensor_scalar(u, w, -0.5, 1.5, ALU.mult, ALU.add))
                line.wait(m)
                m = line.mark(line.eng.tensor_tensor(y, y, u, ALU.mult))
            return m

        def rsqrt_bits(y, v, u, w, ready, line=dve):
            dve.wait(ready)
            m = dve.mark(V.tensor_single_scalar(u.bitcast(I32), v.bitcast(I32), 1, ALU.arith_shift_right))
            dve.wait(m)
            m = dve.mark(V.tensor_scalar(y.bitcast(I32), u.bitcast(I32), -1.0, float(0x5F3759DF), ALU.mult, ALU.add))
            return newton(y, v, u, w, 3, m, line)

        def rsqrt_exp(y, v, eps, scale, u, w, ready, line=dve):
            line.wait(ready)
            m = line.mark(line.eng.tensor_scalar(v, v, scale, eps, ALU.mult, ALU.add))
            act.wait(m)
            m = act.mark(C.activation(u, v, ACT.Ln))
            act.wait(m)
            m = act.mark(C.activation(y, u, ACT.Exp, scale=-0.5))
            return newton(y, v, u, w, 1, m, line)

        C.preload_act_table_set("silu_and_others")
        xn = x1
        m_xn = [None] * NT

        def stats_group(t0, t1):
            m = []
            for t in range(t0, t1):
                dve.wait(got_x[t // 4])
                m.append(dve.mark(V.bn_stats(stats[:, t, :], x_in[:, t, :])))
            dve.wait(m[-1])
            m = [dve.mark(V.bn_aggr(mv[:, t, :], stats[:, t, :])) for t in range(t0, t1)]
            dve.wait(m[-1])
            m = dve.mark(V.tensor_scalar(rs_v[:, t0:t1], mv[:, t0:t1, 1], 1e-6, None, ALU.add))
            m = rsqrt_bits(rstd[:, t0:t1], rs_v[:, t0:t1], rs_u[:, t0:t1], mv[:, t0:t1, 1], m)
            dve.wait(m)
            for t in range(t0, t1):
                m_xn[t] = dve.mark(V.tensor_scalar(xn[:, t, :], x_in[:, t, :], mv[:, t, 0:1], rstd[:, t:t + 1],
                                                   ALU.subtract, ALU.mult))

        zo = y[:, :, :, :].rearrange("p b k c -> p (b k c)")[:, 0:2 * S].rearrange("p (i q) -> p i q", i=2)
        pool.mark(G.memset(zo[:, 0, :], 0.0))
        m_zo = pool.mark(G.memset(zo[:, 1, :], 1.0))
        a_init = arrivals("a_init")
        pool.wait(m_zo)
        for i, dram in enumerate((k_dram, q_dram)):
            for b in range(B):
                got_init = a_init.add(nc.gpsimd.dma_start(dram[b, :, 3, :], zo[:, 1 - i, :]))
        m_vals = pool.mark(G.memset(vals[:, :, :, HD:HD + 1], 1.0))
        m_q0 = pool.mark(G.memset(queries[:, :, :, :, :].bitcast(F32), 0.0))
        pool.wait(*got_x)
        m_x2 = pool.mark(G.tensor_scalar(x_twice[:, :, :], x_in[:, :, :], 2.0, None, ALU.mult))

        stats_group(0, 4)
        dve.wait(got_w)
        m_causal = dve.mark(V.tensor_copy(causal_r[:, :], causal))
        m_after = dve.mark(V.tensor_copy(after_r[:, :], after))
        stats_group(4, NT)
        pool.wait(got_w, got_w2)
        m_cb = pool.mark(G.tensor_copy(before_b[:, :], before))
        m_cb = pool.mark(G.memset(ones_b[:, :], 1.0))
        m_cb = pool.mark(G.tensor_copy(ident_r[:, :], ident))
        m_cb = pool.mark(G.memset(count[:, :], 0.0))
        m_cb = pool.mark(G.memset(table[:, :], 0.0))

        freed_hT, freed_tp, freed_mm = [None] * 2, [None] * 2, [None] * 2
        m_hT = [None] * NT
        m_proj = [None] * NT
        m_dts = [None] * NT
        freed_cT, freed_split = [None] * 2, [None] * 2
        a_kw, a_kr = [arrivals("a_kw0"), arrivals("a_kw1")], [arrivals(f"a_kr{i}") for i in range(KR)]
        got_keys, k_written = [None] * B, [None] * B
        m_valsb = [None] * NT

        def turn_normed(t):
            s = t % 2
            pe.wait(got_w, m_xn[t], freed_tp[s])
            m = pe.mark(TE.transpose(bank(s)[:, 0:P], xn[:, t, :], ident))
            act.wait(m, got_w, freed_hT[s])
            m_hT[t] = freed_tp[s] = act.mark(C.activation(hT[:, s, :], bank(s)[:, 0:P], ACT.Identity,
                                                          bias=ln_wb[:, 1:2], scale=ln_wb[:, 0:1]))

        def project(t):
            s = t % 2
            pb = bank(2 + 2 * s, 2)
            pe.wait(m_hT[t], freed_mm[s])
            pe.mark(TE.matmul(pb[:, 0:BANK], hT[:, s, :], w_in[:, 0:BANK], start=True, stop=True))
            m = freed_hT[s] = pe.mark(TE.matmul(pb[:, BANK:DIN], hT[:, s, :], w_in[:, BANK:DIN], start=True, stop=True))
            act.wait(m)
            m_proj[t] = act.mark(C.activation(proj[:, t, :], pb[:, 0:DZ], ACT.Silu))
            dve.wait(m_proj[t])
            m_dts[t] = dve.mark(V.tensor_tensor(dts[:, t, :], pb[:, DZ:DIN], dt_bias[:, :], ALU.add))
            freed_mm[s] = [m_proj[t], m_dts[t]]

        bc = proj[:, :, 2 * DI:DZ].rearrange("p t (m n) -> p t m n", m=2)
        rotv = rot[:, :, :].rearrange("p (t m) n -> p t m n", m=2)
        m_rot = [None] * B

        def rotate(b):
            tt = slice(TPS * b, TPS * b + TPS)
            cos, sin = (rope_cs[:, i, :].rearrange("p (t m n) -> p t m n", t=TPS, m=2) for i in range(2))
            dve.wait(m_proj[TPS * b + 1], got_w2)
            dve.wait(m_rot[b - 1])
            for e in range(2):
                dve.mark(V.tensor_tensor(rsc[:, :, :, e::2], bc[:, tt, :, 1 - e:ROPE:2], sin[:, :, :, e::2], ALU.mult))
            m = dve.mark(V.tensor_tensor(rotv[:, tt, :, 0:ROPE], bc[:, tt, :, 0:ROPE], cos, ALU.mult))
            dve.mark(V.tensor_copy(rotv[:, tt, :, ROPE:NS], bc[:, tt, :, ROPE:NS]))
            dve.wait(m)
            m_rot[b] = dve.mark(V.tensor_tensor(rotv[:, tt, :, 0:ROPE], rotv[:, tt, :, 0:ROPE], rsc[:, :, :, :], ALU.add))

        def turn_context(b):
            s = b % 2
            pe.wait(got_c[b // 4], fr_c["tp"])
            for k in range(TPS):
                m = pe.mark(TE.transpose(bank(6)[:, k * P:(k + 1) * P], ctx_in[:, TPS * b + k, :], ident))
            act.wait(m, freed_cT[s])
            m_cT[b] = act.mark(C.activation(cT[:, s, :], bank(6)[:, 0:S], ACT.Identity))

        def keys_values(b):
            s = b % 2
            pe.wait(m_cT[b], got_w2, fr_c["kp"])
            m = pe.mark(TE.matmul(bank(7)[:, 0:S], wk[:, :], cT[:, s, :], start=True, stop=True))
            for k in range(TPS):
                mv_ = pe.mark(TE.matmul(bank(6)[:, S + k * P:S + (k + 1) * P], cT[:, s, k * P:(k + 1) * P], wv[:, :],
                                       start=True, stop=True))
            freed_cT[s] = mv_
            act.wait(m, freed_split[s])
            mk1 = act.mark(C.activation(split_qk[:, s, 0, :], bank(7)[:, 0:S], ACT.Identity, bias=bqk[:, 1:2]))
            dve.wait(mk1)
            mk2 = fr_c["kp"] = dve.mark(V.scalar_tensor_tensor(
                split_qk[:, s, 1, :], bank(7)[:, 0:S], bqk[:, 1:2], split_qk[:, s, 0, :].bitcast(F32),
                ALU.add, ALU.subtract))
            dve.wait(mv_, m_vals)
            for k in range(TPS):
                t = TPS * b + k
                m_valsb[t] = dve.mark(V.tensor_tensor(
                    vals[:, t, :, 0:HD], bank(6)[:, S + k * P:S + (k + 1) * P].rearrange("p (h d) -> p h d", d=HD),
                    bv[:, :].rearrange("p (h d) -> p h d", d=HD), ALU.add))
            fr_c["tp"] = m_valsb[t]
            sp.wait(mk1, mk2)
            head, rest = (split_qk[:, s, i, :].bitcast(F32) for i in range(2))
            a_kw[s].add(nc.sync.dma_start(k_dram[b, :, 0:3:2, :], head.unsqueeze(1).to_broadcast([P, 2, S])))
            freed_split[s] = a_kw[s].add(nc.sync.dma_start(k_dram[b, :, 1, :], rest))
            k_written[b] = freed_split[s]

        fr_c, m_cT = {"tp": None, "kp": None}, [None] * B
        for i in range(NT + 1):
            if i < NT:
                turn_normed(i)
            if i >= 1:
                project(i - 1)
            if i % 2 == 1:
                turn_context(i // 2)
            elif i >= 2:
                keys_values(i // 2 - 1)
                rotate(i // 2 - 1)

        C.preload_act_table_set("natural_log_exp_and_others")
        flat = dts[:, :, :].rearrange("p t h -> p (t h)")
        dve.wait(m_dts[NT - 1])
        m = dve.mark(V.scalar_tensor_tensor(sp_d[:, :], flat, -1.0, flat, ALU.mult, ALU.min))
        act.wait(m, m_one)
        m_e = act.mark(C.activation(sp_e[:, :], sp_d[:, :], ACT.Exp))
        act.wait(m_e)
        m_l = act.mark(C.activation(sp_l[:, :], sp_e[:, :], ACT.Ln, bias=one[:, :]))
        dve.wait(m_e)
        m = dve.mark(V.tensor_scalar(sp_d[:, :], sp_e[:, :], 1.0, -1.0, ALU.add, ALU.add))
        dve.wait(m)
        m = dve.mark(V.tensor_single_scalar(sp_q[:, :], sp_d[:, :], 0.0, ALU.is_equal))
        dve.wait(m, m_l)
        dve.mark(V.tensor_tensor(sp_l[:, :], sp_l[:, :], sp_q[:, :], ALU.add))
        m = dve.mark(V.tensor_tensor(sp_d[:, :], sp_d[:, :], sp_q[:, :], ALU.add))
        dve.wait(m)
        m = dve.mark(V.reciprocal(sp_q[:, :], sp_d[:, :]))
        dve.wait(m)
        m = dve.mark(V.tensor_tensor(sp_l[:, :], sp_l[:, :], sp_q[:, :], ALU.mult))
        dve.wait(m)
        m = dve.mark(V.tensor_tensor(sp_l[:, :], sp_l[:, :], sp_e[:, :], ALU.mult))
        dve.wait(m)
        m_dt = dve.mark(V.scalar_tensor_tensor(flat, flat, 0.0, sp_l[:, :], ALU.max, ALU.add))
        act.wait(got_w2)
        m = act.mark(C.activation(neg_a[:, :], neg_a[:, :], ACT.Exp))
        dve.wait(m, m_dt)
        m = dve.mark(V.scalar_tensor_tensor(a_raw[:, :, :], dts[:, :, :], -1.0,
                                            neg_a[:, :].unsqueeze(1).to_broadcast([P, NT, NH]), ALU.mult, ALU.mult))
        dve.wait(m)
        m = dve.mark(V.tensor_copy(a_hi[:, :, :], a_raw[:, :, :]))
        dve.wait(m)
        m_a = dve.mark(V.tensor_tensor(a_lo[:, :, :], a_raw[:, :, :], a_hi[:, :, :].bitcast(F32), ALU.subtract))
        pe.wait(m_a, m_after, m_causal, *freed_mm)
        for w, c0 in ((causal_r, 0), (after_r, NT * NH)):
            for part, a in enumerate((a_hi, a_lo)):
                m = pe.mark(TE.matmul(bank(2)[:, c0:c0 + NT * NH], w[:, :], a[:, :, :].rearrange("p t h -> p (t h)"),
                                     start=part == 0, stop=part == 1))
        act.wait(m)
        act.mark(C.activation(ecs[:, :, :].rearrange("p t h -> p (t h)"), bank(2)[:, 0:NT * NH], ACT.Exp))
        m_dec = act.mark(C.activation(dec[:, :, :].rearrange("p t h -> p (t h)"),
                                      bank(2)[:, NT * NH:2 * NT * NH], ACT.Exp))
        pool.wait(got_w2)
        for c in range(2):
            m_wo = pool.mark(G.tensor_scalar(w_out[:, c, :], w_out[:, c, :], rms_w[:, c:c + 1], None, ALU.mult))

        work = ctx_in[:, :, :].rearrange("p t d -> p (t d)")
        decay = work[:, 0:3 * NH * P].rearrange("p (r h l) -> p r h l", r=3, h=NH)
        score = work[:, 3 * NH * P:(3 * NH + 2) * P].rearrange("p (r l) -> p r l", r=2)

        yT = w_in[:, 0:TPS * 2 * P].rearrange("p (k c l) -> p k c l", k=TPS, c=2)
        x1T = x2T = cT[:, 1, :]
        free = {("y", 0): got_init}
        m_bcT, m_dcy, m_xdt, m_skip, m_xdec, m_mat, m_y, m_sq = ({} for _ in range(8))

        m_seg = {}

        def mask_decays(t):
            s = t % 3
            m_seg[t] = []
            for eng, part, a in ((dve, 0, a_hi), (pool, 1, a_lo)):
                eng.wait(m_a, m_causal, free.get(("seg", s)))
                m = eng.mark(eng.eng.tensor_tensor(
                    seg[:, s, part], causal.unsqueeze(1).to_broadcast([P, NH, P]),
                    a[:, t, :].bitcast(F32).unsqueeze(2).to_broadcast([P, NH, P]), ALU.mult))
                m_seg[t].append(m)

        def scale_inputs(t):
            r = t % 4
            xs = proj[:, t, DI:2 * DI].rearrange("p (h c) -> p h c", h=NH)
            pool.wait(m_dt, free.get(("xdt", r)))
            m = m_xdt[t] = pool.mark(G.tensor_tensor(
                xdt[:, r], xs, dts[:, t, :].unsqueeze(2).to_broadcast([P, NH, HP]), ALU.mult))
            pool.wait(free.get(("skip", r)))
            m_skip[t] = pool.mark(G.tensor_tensor(
                skip[:, r], xs, d_skip[:, :].unsqueeze(2).to_broadcast([P, NH, HP]), ALU.mult))
            if t % TPS == 0:
                pool.wait(m, m_dec, free.get(("xdec", (t // TPS) % 2)))
                m_xdec[t] = pool.mark(G.tensor_tensor(
                    xdec[:, (t // TPS) % 2], xdt[:, r], dec[:, t, :].unsqueeze(2).to_broadcast([P, NH, HP]), ALU.mult))

        def mix_exps(t):
            s, r = t % 2, t % 3
            pe.wait(m_seg[t], free.get(("segbank", s)), m_dec)
            for part in range(2):
                m = pe.mark(TE.matmul(bank(s), after_r[:, :], seg[:, t % 3, part].rearrange("p h l -> p (h l)"),
                                     start=part == 0, stop=part == 1))
            free["seg", t % 3] = m
            act.wait(m, free.get(("decay", r)))
            m_dcy[t] = free["segbank", s] = act.mark(C.activation(decay[:, r].rearrange("p h l -> p (h l)"), bank(s), ACT.Exp))
            pe.wait(m_rot[t // TPS], free.get("bcbank"))
            for i in range(2):
                m = pe.mark(TE.transpose(bank(2)[0:NS, i * P:(i + 1) * P], rot[:, 2 * t + i, :], ident))
            act.wait(m, free.get(("bcT", r)))
            m_bcT[t] = act.mark(C.activation(bcT[:, r].rearrange("p i l -> p (i l)"), bank(2)[0:NS, 0:2 * P], ACT.Identity))

        def mix_matrix(t):
            s, r = t % 2, t % 3
            pe.wait(m_bcT[t])
            m = pe.mark(TE.matmul(bank(2)[:, 2 * P:3 * P], bcT[:, r, 0, :], bcT[:, r, 1, :], start=True, stop=True))
            dve.wait(m)
            m = free["bcbank"] = dve.mark(V.tensor_tensor(score[:, s, :], bank(2)[:, 2 * P:3 * P], causal, ALU.mult))
            dve.wait(m, m_dcy[t])
            m_mat[t] = dve.mark(V.tensor_tensor(decay[:, r], decay[:, r],
                                                score[:, s, :].unsqueeze(1).to_broadcast([P, NH, P]), ALU.mult))

        def mix(t):
            k, r, q, bb = t % TPS, t % 3, t % 4, (t // TPS) % 2
            if k == 0:
                pe.wait(m_xdec[t], free.get("offbank"))
                m_st = free["xdec", bb] = pe.mark(TE.matmul(bank(4)[0:NS, 0:DI], rot[:, 2 * t, :],
                                                       xdec[:, bb].rearrange("p h c -> p (h c)"), start=True, stop=True))
                act.wait(m_st, free.get("state"))
                m_state = free["offbank"] = act.mark(C.activation(state[:, :], bank(4)[0:NS, 0:DI], ACT.Identity))
                free["m_state"] = m_state
                add, m_add = skip[:, q].rearrange("p h c -> p (h c)"), m_skip[t]
            else:
                pe.wait(free["m_state"], free.get("offbank"))
                m_off = free["state"] = pe.mark(TE.matmul(bank(4)[:, 0:DI], bcT[:, r, 1, :], state[:, :],
                                                         start=True, stop=True))
                dve.wait(m_off, m_dec)
                m2 = free["offbank"] = dve.mark(V.tensor_tensor(
                    yoff[:, :].rearrange("p (h c) -> p h c", h=NH), bank(4)[:, 0:DI].rearrange("p (h c) -> p h c", h=NH),
                    ecs[:, t, :].unsqueeze(2).to_broadcast([P, NH, HP]), ALU.mult))
                dve.wait(m2, m_skip[t])
                m_add = dve.mark(V.tensor_tensor(yoff[:, :], yoff[:, :], skip[:, q].rearrange("p h c -> p (h c)"), ALU.add))
                add = yoff[:, :]
            pe.wait(m_mat[t], m_xdt[t], free.get("ybank"))
            for h in range(NH):
                m = pe.mark(TE.matmul(bank(3)[:, h * HP:(h + 1) * HP], decay[:, r, h, :], xdt[:, q, h, :],
                                     start=True, stop=True))
            free["decay", r] = free["bcT", r] = m
            free["xdt", q] = [m, m_xdec.get(t)]
            dve.wait(m, m_add, free.get(("y", bb)))
            m = free["ybank"] = free["skip", q] = dve.mark(V.tensor_tensor(y[:, bb, k, :], bank(3)[:, 0:DI], add, ALU.add))
            pool.wait(m)
            m = m_y[t] = pool.mark(G.tensor_tensor(y[:, bb, k, :], y[:, bb, k, :], proj[:, t, 0:DI], ALU.mult))

        def mix_square(t):
            k, bb = t % TPS, (t // TPS) % 2
            act.wait(m_y[t], free.get(("ss", bb)), m_sq.get(t - 1))
            m_sq[t] = act.mark(C.activation(ysq[:, :], y[:, bb, k, :], ACT.Square, accum_out=ss[:, 0, bb, k:k + 1]))

        m_o, m_bn, m_rs1, m_x1, m_ln1 = ({} for _ in range(5))

        m_yT = {}

        def turn_mixed(b):
            bb = b % 2
            pe.wait(m_y[TPS * b + 1], free.get("yTbank"))
            for k in range(TPS):
                for c in range(2):
                    m = pe.mark(TE.transpose(bank(5)[:, (2 * k + c) * P:(2 * k + c + 1) * P],
                                            y[:, bb, k, c * P:(c + 1) * P], ident))
            free["y", bb] = [m, m_sq[TPS * b + 1]]
            act.wait(m, free.get("yT"))
            m_yT[b] = free["yTbank"] = act.mark(C.activation(yT[:, :, :, :].rearrange("p k c l -> p (k c l)"), bank(5), ACT.Identity))
            m_rs1[b] = rsqrt_exp(ss[:, 1, bb], ss[:, 0, bb], 1e-6, 1.0 / DI, ss[:, 2, bb], ss[:, 3, bb],
                                 m_sq[TPS * b + 1], pool)

        def mix_project(b):
            pe.wait(m_yT[b], m_wo, free.get("obank"))
            for k in range(TPS):
                for c in range(2):
                    m = pe.mark(TE.matmul(bank(6)[:, k * D:(k + 1) * D], yT[:, k, c, :], w_out[:, c, :],
                                         start=c == 0, stop=c == 1))
            free["yT"] = m_o[b] = m

        def mix_residual(b):
            bb = b % 2
            dve.wait(m_rs1[b], m_o[b], m_x2, free.get(("r1", bb)), free.get("st1"))
            for k in range(TPS):
                m = dve.mark(V.scalar_tensor_tensor(r1[:, bb, k, :], bank(6)[:, k * D:(k + 1) * D], ss[:, 1, bb, k:k + 1],
                                                    x_twice[:, TPS * b + k, :], ALU.mult, ALU.add))
            free["obank"] = free["ss", bb] = m
            dve.wait(m)
            m = [dve.mark(V.bn_stats(st1[:, k, :], r1[:, bb, k, :])) for k in range(TPS)][-1]
            dve.wait(m)
            m = [dve.mark(V.bn_aggr(mv1[:, bb, k, :], st1[:, k, :])) for k in range(TPS)][-1]
            m_ln1[b] = rsqrt_exp(nw[:, 0, bb], mv1[:, bb, :, 1], 1e-5, 1.0, nw[:, 1, bb], nw[:, 2, bb], m, pool)

        def mix_norm(b):
            bb = b % 2
            dve.wait(m_ln1[b])
            for k in range(TPS):
                m_x1[b] = free["r1", bb] = dve.mark(V.tensor_scalar(
                    x1[:, TPS * b + k, :], r1[:, bb, k, :], mv1[:, bb, k, 0:1], nw[:, 0, bb, k:k + 1],
                    ALU.subtract, ALU.mult))

        a_qw, a_qr = [arrivals("a_qw0"), arrivals("a_qw1")], [[arrivals(f"a_qr{i}_{j}") for j in range(GJ)] for i in range(2)]
        got_q, q_written, m_x1T = {}, [None] * B, {}

        def turn_x1(b):
            pe.wait(m_x1[b], free.get("misc"), m_valsb[NT - 1])
            for k in range(TPS):
                m = pe.mark(TE.transpose(bank(7)[:, k * P:(k + 1) * P], x1[:, TPS * b + k, :], ident))
            act.wait(m, free.get("x1T"))
            m_x1T[b] = free["misc"] = act.mark(C.activation(x1T[:, :], bank(7)[:, 0:S], ACT.Identity))

        def query(b):
            s = b % 2
            pe.wait(m_x1T[b], free["misc"])
            m = free["x1T"] = pe.mark(TE.matmul(bank(7)[:, S:2 * S], wq[:, :], x1T[:, :], start=True, stop=True))
            act.wait(m, freed_split[s])
            m1 = act.mark(C.activation(split_qk[:, s, 0, :], bank(7)[:, S:2 * S], ACT.Identity, bias=bqk[:, 0:1]))
            dve.wait(m1)
            m2 = free["misc"] = dve.mark(V.scalar_tensor_tensor(
                split_qk[:, s, 1, :], bank(7)[:, S:2 * S], bqk[:, 0:1], split_qk[:, s, 0, :].bitcast(F32),
                ALU.add, ALU.subtract))
            sp.wait(m1, m2)
            head, rest = (split_qk[:, s, i, :].bitcast(F32) for i in range(2))
            a_qw[s].add(nc.sync.dma_start(q_dram[b, :, 0:2, :], head.unsqueeze(1).to_broadcast([P, 2, S])))
            q_written[b] = freed_split[s] = a_qw[s].add(nc.sync.dma_start(q_dram[b, :, 2, :], rest))

        probs = work.rearrange("p (n k q) -> p n k q", n=4, k=TPS)
        a_mw, a_mr = [arrivals("a_mw0"), arrivals("a_mw1")], [[arrivals(f"a_mr{i}_{j}") for j in range(GJ)] for i in range(2)]
        SCALE = 1.0 / float(np.sqrt(np.float32(HD)))
        freed_q, freed_k = {}, [None] * KR
        m_max, got_max, m_x2d, m_av = {}, {}, {}, {}
        MISC = bank(7)

        def load_keys(b):
            s = b % KR
            sp.wait(k_written[b], got_init, freed_k[s])
            for j in range(GJ):
                src = k_dram[b, 32 * j:32 * j + 32].rearrange("(r d) c q -> (d c) r q", r=GR)
                got_keys[b] = a_kr[s].add(nc.sync.dma_start(keys[32 * j:32 * j + 32, s, :, :].bitcast(F32), src))

        def load_queries(b, j):
            s = b % 2
            sp.wait(q_written[b], got_init, m_q0, freed_q.get((b - 2, j)))
            src = q_dram[b, 32 * j:32 * j + 32].rearrange("(r d) c q -> (d c) r q", r=GR)
            got_q[b, j] = a_qr[s][j].add(nc.sync.dma_start(queries[32 * j:32 * j + 32, s, :, j, :].bitcast(F32), src))

        def maxima(b, h, n):
            s, j, r, bk = b % 2, h // GR, h % GR, bank(n % 2)
            pe.wait(got_q[b, j], got_keys[b], free.get(("abank", n % 2)))
            for k in range(TPS):
                m = pe.mark(TE.matmul(bk[:, k * S:(k + 1) * S], queries[:, s, r, j, k * P:(k + 1) * P],
                                     keys[:, b % KR, r, :], start=True, stop=True))
            dve.wait(m, free.get(("nm", s)))
            free["abank", n % 2] = m_max[b] = dve.mark(V.tensor_reduce(
                nm[:, s, :, h], bk.rearrange("p (k q) -> p k q", k=TPS), AX_X, ALU.max, negate=True))

        def maxima_out(b):
            s = b % 2
            pe.wait(m_max[b], free.get("misc"))
            for k in range(TPS):
                m = free["nm", s] = pe.mark(TE.transpose(MISC[0:AH, k * P:(k + 1) * P], nm[:, s, k, :], ident))
            act.wait(m, free.get("nm12"))
            m1 = act.mark(C.activation(nm12[:, 0, :], MISC[0:AH, 0:S], ACT.Identity))
            dve.wait(m1)
            m2 = free["misc"] = dve.mark(V.tensor_tensor(nm12[:, 1, :], MISC[0:AH, 0:S],
                                                         nm12[:, 0, :].bitcast(F32), ALU.subtract))
            sp.wait(m1, m2)
            dst = q_dram[b].rearrange("(h d) c q -> h d c q", d=HD)[:, 0:2, 3, :]
            m = free["nm12"] = a_mw[s].add(nc.sync.dma_start(dst, nm12[:, :, :].bitcast(F32)))
            sp.wait(m, m_max[b])
            for j in range(GJ):
                src = q_dram[b, 32 * j:32 * j + 32].rearrange("(r d) c q -> d c r q", r=GR)[0:2, 3]
                got_max[b, j] = a_mr[s][j].add(nc.sync.dma_start(
                    queries[32 * j + 3:32 * j + 8:4, s, :, j, :].bitcast(F32), src))

        mask_decays(0)
        scale_inputs(0)
        mask_decays(1)
        LAGS = ((query, 14), (turn_x1, 12), (mix_norm, 10), (mix_residual, 7), (mix_project, 6), (turn_mixed, 5))

        FIRST = 2

        def mixer_steps():
            for i in range(NT + LAGS[0][1] - 1):
                for stage, lag in LAGS:
                    b, odd = divmod(i - lag, 2)
                    if not odd and 0 <= b < B:
                        stage(b)
                for stage, lag in ((mix_square, 3), (mix, 2), (mix_matrix, 1), (mix_exps, 0), (scale_inputs, -1), (mask_decays, -2)):
                    if 0 <= i - lag < NT:
                        stage(i - lag)
                if i in (8, 10):
                    load_keys((i - 8) // 2)
                if i in (15, 17):
                    for j in range(GJ):
                        load_queries((i - 15) // 2, j)
                if i == NT:
                    pe.wait(free["segbank", 0], free["segbank", 1])
                if NT <= i < NT + FIRST:
                    for h in range(AH * (i - NT) // FIRST, AH * (i - NT + 1) // FIRST):
                        maxima(0, h, h)
                if i == NT + FIRST:
                    maxima_out(0)
                yield

        steps = mixer_steps()
        for _ in range(NT + 6):
            next(steps)

        m_exp = {}

        def exps(b, h):
            n = AH * b + h
            s, j, r, bk, e = b % 2, h // GR, h % GR, bank(2 + n % 3), n % 4
            pe.wait(got_max[b, j], free.get(("bbank", n % 3)))
            for k in range(TPS):
                m = pe.mark(TE.matmul(bk[:, k * S:(k + 1) * S], keys[:, b % KR, r, k * P:(k + 1) * P],
                                     queries[:, s, r, j, :], start=True, stop=True))
            freed_q[b, j] = freed_k[b % KR] = m
            act.wait(m, free.get(("probs", e)))
            m_exp[n] = free["bbank", n % 3] = act.mark(C.activation(
                probs[:, e].rearrange("p k q -> p (k q)"), bk, ACT.Exp, scale=SCALE))

        def weigh(n):
            b, h = divmod(n, AH)
            pe.wait(m_exp[n], free.get("avbank"))
            p0, c0 = 32 * (h % 4), (h // 4) * S
            for k in range(TPS):
                m = pe.mark(TE.matmul(bank(5, 2)[p0:p0 + HD + 1, c0:c0 + S], vals[:, TPS * b + k, h, :],
                                     probs[:, n % 4, k, :], start=k == 0, stop=k == 1, tile_position=(0, p0)))
            free["probs", n % 4] = m
            m_av[b] = m

        avT = y[:, :, :, :].rearrange("p b k c -> p (b k c)")
        x2 = x_in
        oT = w_in[:, S:2 * S]
        r2 = w_in[:, 0:S].rearrange("p (k d) -> p k d", k=TPS)
        x1b = cT[:, 0, :].rearrange("p (k d) -> p k d", k=TPS)

        def attention_out(b):
            act.wait(m_av[b], free.get("avT"))
            m1 = act.mark(C.activation(avT[:, 0:BANK], bank(5), ACT.Identity))
            dve.wait(m_av[b], free.get("avT"))
            m2 = dve.mark(V.tensor_copy(avT[:, BANK:], bank(6)))
            free["avbank"] = [m1, m2]
            pool.wait(m_x1[b], free.get("x1b"))
            m_xb = pool.mark(G.tensor_tensor(x1b, x1[:, TPS * b:TPS * b + TPS, :],
                                             bo[:, :].unsqueeze(1).to_broadcast([P, TPS, D]), ALU.add))
            yield
            for q in range(TPS):
                pe.wait(m1, m2, free.get("misc"))
                for g in range(4):
                    m = pe.mark(TE.transpose(MISC[:, g * P:(g + 1) * P], avT[:, g * S + q * P:g * S + (q + 1) * P], ident))
                free["avT"] = m
                av = MISC.rearrange("p (h c) -> p h c", c=32)
                dve.wait(m, free.get("rec"))
                m = dve.mark(V.reciprocal(rec[:, :], av[:, :, HD]))
                dve.wait(m, free.get("o_sb"))
                m_on = free["misc"] = free["rec"] = dve.mark(V.tensor_tensor(
                    o_sb[:, q, :].rearrange("p (h d) -> p h d", d=HD), av[:, :, 0:HD],
                    rec[:, :].unsqueeze(2).to_broadcast([P, AH, HD]), ALU.mult))
                yield
            pe.wait(m_on)
            for k in range(TPS):
                m = pe.mark(TE.transpose(MISC[:, k * P:(k + 1) * P], o_sb[:, k, :], ident))
            free["o_sb"] = m
            act.wait(m, free.get("oT"))
            m_oT = free["misc"] = act.mark(C.activation(oT, MISC[:, 0:S], ACT.Identity))
            yield
            pe.wait(m_oT, free.get("misc"))
            for k in range(TPS):
                m = free["oT"] = pe.mark(TE.matmul(MISC[:, k * P:(k + 1) * P], oT[:, k * P:(k + 1) * P], wo[:, :],
                                                  start=True, stop=True))
            dve.wait(m, m_xb, free.get("r2"))
            m = free["x1b"] = free["misc"] = dve.mark(V.tensor_tensor(
                r2.rearrange("p k d -> p (k d)"), MISC[:, 0:S], x1b.rearrange("p k d -> p (k d)"), ALU.add))
            dve.wait(m)
            m = [dve.mark(V.bn_stats(st2[:, k, :], r2[:, k, :])) for k in range(TPS)][-1]
            dve.wait(m)
            m = [dve.mark(V.bn_aggr(mv2[:, k, :], st2[:, k, :])) for k in range(TPS)][-1]
            yield
            m = rsqrt_exp(nw2[:, 0, :], mv2[:, :, 1], 1e-5, 1.0, nw2[:, 1, :], nw2[:, 2, :], m, pool if b < B - 1 else dve)
            yield
            dve.wait(m, m_x2)
            for k in range(TPS):
                m = free["r2"] = dve.mark(V.tensor_scalar(
                    x2[:, TPS * b + k, :], r2[:, k, :], mv2[:, k, 0:1], nw2[:, 0, k:k + 1], ALU.subtract, ALU.mult))
            m_x2d[b] = m
            yield
            yield from route(b)

        a_x2 = arrivals("a_split")
        m_route, m_diff = {}, {}

        def route(b):
            s = b % 2
            tt = slice(TPS * b, TPS * b + TPS)
            act.wait(m_x2d[b], free.get("x2_split"))
            m = act.mark(C.activation(x2_split[:, :, 0, :], x2[:, tt, :], ACT.Identity))
            pool.wait(m)
            m = pool.mark(G.tensor_tensor(x2_split[:, :, 1, :], x2[:, tt, :], x2_split[:, :, 0, :].bitcast(F32),
                                          ALU.subtract))
            sp.wait(m)
            free["x2_split"] = a_x2.add(nc.sync.dma_start(
                x2_dram[b * S:(b + 1) * S].rearrange("(k p) c -> p k c", p=P),
                x2_split[:, :, :, :].rearrange("p k i d -> p k (i d)").bitcast(F32)))
            pe.wait(m_x2d[b], free.get("misc"))
            for k in range(TPS):
                m = pe.mark(TE.transpose(MISC[:, k * P:(k + 1) * P], x2[:, TPS * b + k, :], ident))
            act.wait(m, free.get("x2T"))
            m = free["misc"] = act.mark(C.activation(x2T[:, :], MISC[:, 0:S], ACT.Identity))
            yield
            pe.wait(m, free.get("misc"))
            for k in range(TPS):
                m = pe.mark(TE.matmul(MISC[:, k * NE:(k + 1) * NE], x2T[:, k * P:(k + 1) * P], gate[:, :],
                                      start=True, stop=True))
            free["x2T"] = m
            dve.wait(m, m_route.get("logit"))
            m = free["misc"] = dve.mark(V.tensor_copy(logit[:, :, :].rearrange("p t e -> p (t e)"), MISC[:, 0:TPS * NE]))
            dve.wait(m)
            for k in range(TPS):
                m = dve.mark(V.max(top[:, k, :], logit[:, k, :]))
            dve.wait(m)
            for k in range(TPS):
                m = m_route["logit"] = dve.mark(V.max_index(topi[:, k, :], top[:, k, :], logit[:, k, :]))
            dve.wait(m)
            m_diff[b] = dve.mark(V.tensor_tensor(wgt[:, tt, 1], top[:, :, 1], top[:, :, 0], ALU.subtract))
            m = dve.mark(V.tensor_copy(topf[:, :, :], topi[:, :, :]))
            dve.wait(m, m_route.get("picked"))
            yield
            for k in range(TOPK):
                m = dve.mark(V.tensor_tensor(choice[:, k], iota[:, 0:NE].unsqueeze(1).to_broadcast([P, TPS, NE]),
                                             topf[:, :, k].unsqueeze(2).to_broadcast([P, TPS, NE]), ALU.is_equal))
            dve.wait(m, m_route.get("counted"))
            m = dve.mark(V.tensor_tensor(chosen[:, :, :], choice[:, 0], choice[:, 1], ALU.add))
            yield
            pe.wait(m, m_cb, free.get("misc"))
            for t in range(TPS):
                for u in range(t):
                    pe.mark(TE.matmul(MISC[:, t * NE:(t + 1) * NE], ones_b[:, :], chosen[:, u, :], start=u == 0, stop=False))
                pe.mark(TE.matmul(MISC[:, t * NE:(t + 1) * NE], before_b[:, :], chosen[:, t, :], start=t == 0, stop=True))
            for t in range(TPS):
                m = pe.mark(TE.matmul(MISC[:, TPS * NE:(TPS + 1) * NE], ones_b[:, :], chosen[:, t, :],
                                      start=t == 0, stop=t == TPS - 1))
            m_route["counted"] = m
            dve.wait(m, m_cb, m_route.get("count"))
            m = dve.mark(V.tensor_tensor(rank[:, :, :], MISC[:, 0:TPS * NE].rearrange("p (t e) -> p t e", e=NE),
                                         count[:, :].unsqueeze(1).to_broadcast([P, TPS, NE]), ALU.add))
            dve.wait(m)
            m_route["count"] = free["misc"] = dve.mark(V.tensor_tensor(
                count[:, :], count[:, :], MISC[:, TPS * NE:(TPS + 1) * NE], ALU.add))
            m = dve.mark(V.tensor_tensor(picked[:, :, :, :], choice[:, :, :, :],
                                         rank[:, :, :].unsqueeze(1).to_broadcast([P, TOPK, TPS, NE]), ALU.mult))
            dve.wait(m)
            m = m_route["picked"] = dve.mark(V.tensor_reduce(
                place[:, :], picked[:, :, :, :].rearrange("p k t e -> p (k t) e"), AX_X, ALU.add))
            yield
            dve.wait(m)
            m = dve.mark(V.tensor_copy(place_i[:, :], place[:, :]))
            dve.wait(m)
            dve.mark(V.tensor_single_scalar(part_i[:, 0, :], place_i[:, :], P - 1, ALU.bitwise_and))
            m = dve.mark(V.tensor_single_scalar(part_i[:, 1, :], place_i[:, :], P.bit_length() - 1, ALU.arith_shift_right))
            dve.wait(m, m_route.get("hot"))
            m = dve.mark(V.tensor_copy(part_f[:, :, :], part_i[:, :, :]))
            dve.wait(m)
            m = dve.mark(V.scalar_tensor_tensor(column[:, :].rearrange("p (k t) -> p k t", k=TOPK),
                                                topf[:, :, 0:TOPK].rearrange("p t k -> p k t"), float(LT),
                                                part_f[:, 1, :].rearrange("p (k t) -> p k t", k=TOPK), ALU.mult, ALU.add))
            yield
            rows_on = pool if b == B - 1 else dve
            for line in (dve, rows_on):
                line.wait(m, m_route.get("spread"))
            for i in range(TOPK * TPS):
                k, t = divmod(i, TPS)
                m_row = rows_on.mark(rows_on.eng.tensor_scalar(row_hot[:, i, :], iota, part_f[:, 0, i:i + 1], None, ALU.is_equal))
                dve.mark(V.tensor_scalar(col_hot[:, i, 0, :], iota, column[:, i:i + 1], token_no, ALU.is_equal, ALU.mult))
                m = dve.mark(V.tensor_scalar(col_hot[:, i, 1, :], iota, column[:, i:i + 1], float(k * NT + TPS * b + t),
                                             ALU.is_equal, ALU.mult))
                yield
            m_route["hot"] = m = [m, m_row]
            pe.wait(m, free.get("misc"))
            for i in range(TOPK * TPS):
                m = pe.mark(TE.matmul(MISC[:, 0:2 * P], row_hot[:, i, :], col_hot[:, i].rearrange("p i c -> p (i c)"),
                                      start=i == 0, stop=i == TOPK * TPS - 1))
            m_route["spread"] = m
            dve.wait(m, m_cb, m_route.get("table"))
            m = dve.mark(V.tensor_tensor(table[:, :], MISC[:, 0:P], table[:, :], ALU.add))
            dve.wait(m)
            m_route["table"] = free["misc"] = dve.mark(V.scalar_tensor_tensor(
                table[:, :], MISC[:, P:2 * P], float(P), table[:, :], ALU.mult, ALU.add))
            yield

        mixer.close()
        w_split = sb("w_split", [P, NE, W_ALL], F32R)
        mixer_end = []
        w_raw = x_twice[:, :, :].rearrange("p t d -> p (t d)").rearrange("p (r n) -> p r n", n=FF)
        W_RING = NT * D // FF
        a_e = [arrivals(f"a_e{i}") for i in range(W_RING)]
        got_e, m_split = {}, {}
        PIECES = 3 * NE

        def load_weights(n):
            e, i = divmod(n, 3)
            r = n % W_RING
            sp.wait(*(mixer_end if n < W_RING else [m_split[n - W_RING]]))
            if i < 2:
                got_e[n] = a_e[r].add(nc.sync.dma_start(w_raw[:, r, :], A[f"L0_ffn_w{i}"][e]))
            else:
                got_e[n] = a_e[r].add(nc.sync.dma_start(w_raw[:, r, :].rearrange("p (c d) -> p c d", c=FC),
                                                        A["L0_ffn_wo"][e].rearrange("(c p) d -> p c d", p=P)))

        def split_weights(n):
            e, i = divmod(n, 3)
            raw = w_raw[:, n % W_RING, :]
            if i < 2:
                head, rest = (w_split[:, e, c + i * FF:c + (i + 1) * FF] for c in (W_HEAD, W_REST))
            else:
                raw = raw.rearrange("p (c d) -> p c d", c=FC)
                head, rest = (w_split[:, e, W_OUT:].rearrange("p (c h d) -> p c h d", c=FC, h=2)[:, :, h, :] for h in range(2))
            act.wait(got_e[n], *mixer_end)
            m = act.mark(C.activation(head, raw, ACT.Identity))
            pool.wait(m)
            m_split[n] = pool.mark(G.tensor_tensor(rest, raw, head.bitcast(F32), ALU.subtract))
            if n + W_RING < PIECES:
                load_weights(n + W_RING)

        mixer_done = [free[k] for k in (("segbank", 0), ("segbank", 1), "bcbank", "ybank", "offbank", "yTbank", "obank")]
        pe.wait(*mixer_done[:5])
        dve.wait(*mixer_done)
        free["avbank"] = dve.mark(V.memset(bank(5, 2), 0.0))
        na = AH
        LAG = 2
        MAX_FROM, MAX_STEPS = 2, 8
        tail = iter(())
        piece = 0
        for b in range(B):
            for h in range(AH):
                exps(b, h)
                n = h - MAX_FROM
                if b + 1 < B and 0 <= n < MAX_STEPS:
                    for hh in range(AH * n // MAX_STEPS, AH * (n + 1) // MAX_STEPS):
                        maxima(b + 1, hh, na)
                        na += 1
                if AH * b + h >= LAG:
                    weigh(AH * b + h - LAG)
                if b and h == LAG - 1:
                    for _ in tail:
                        pass
                    tail = attention_out(b - 1)
                if b + 1 < B and n == MAX_STEPS:
                    maxima_out(b + 1)
                if b + 2 < B and h == 2:
                    load_keys(b + 2)
                if b + 2 < B and h % GR == GR - 1:
                    load_queries(b + 2, h // GR)
                for _ in range(1 if b + 1 < B else 2):
                    next(tail, None)
                if h % 2 == 0:
                    next(steps, None)
                if b == 1 and h == 0:
                    mixer_end += [(line.sem, line.n) for line in (pe, dve, act, pool)] + freed_split + [got_init]
                    for n in range(W_RING):
                        load_weights(n)
                elif b and h % 4 == 2 and piece < PIECES:
                    split_weights(piece)
                    piece += 1
        for n in range(AH * B - LAG, AH * B):
            weigh(n)
        for _ in tail:
            pass
        for _ in attention_out(B - 1):
            pass

        
        used = sb("used", [P, 1])
        used_b = sb("used_b", [P, 1], BF16)
        slot_tile = sb("slot_tile", [P, 1])
        y_flat = y[:, :, :, :].rearrange("p b k c -> p (b k c)")
        to_slots, slots = (y_flat[:, 3 * D + i * SLOT_TILES:3 * D + (i + 1) * SLOT_TILES] for i in range(2))
        gather_i = sb("gather_i", [P, SLOT_TILES], I32)
        scatter_u = sb("scatter_u", [P, SLOT_TILES], U32)
        weights_at = sb("weights_at", [P, SLOT_TILES], U32)
        tableT, y_half = o_sb[:, 0, :], o_sb[:, 1, :]
        attention_end = [(line.sem, line.n) for line in (pe, dve, act)]
        pe.wait(m_route["table"], free["misc"], *attention_end)
        m = pe.mark(TE.transpose(bank(0)[:, 0:P], table[:, :], ident))
        act.wait(m)
        m_tT = act.mark(C.activation(tableT, bank(0)[:, 0:P], ACT.Identity))
        dve.wait(m_tT)
        dve.mark(V.tensor_single_scalar(used[:, :], tableT[:, 0:1], 0.0, ALU.is_gt))
        m = dve.mark(V.tensor_single_scalar(used_b[:, :], tableT[:, 0:1], 0.0, ALU.is_gt))
        pe.wait(m)
        m = pe.mark(TE.matmul(bank(1)[:, 0:1], before_b[:, :], used_b[:, :], start=True, stop=True))
        dve.wait(m)
        m = dve.mark(V.tensor_copy(slot_tile[:, :], bank(1)[:, 0:1]))
        dve.wait(m)
        m = dve.mark(V.tensor_scalar(to_slots, iota[:, 0:SLOT_TILES], slot_tile[:, :], used[:, :],
                                     ALU.is_equal, ALU.mult))
        pe.wait(m, m_tT)
        m = pe.mark(TE.matmul(bank(2)[:, 0:SLOT_TILES], tableT, to_slots, start=True, stop=True))
        m1 = pe.mark(TE.matmul(bank(3)[:, 0:SLOT_TILES], expert_offset, to_slots, start=True, stop=True))
        dve.wait(m)
        m = dve.mark(V.tensor_scalar(gather_i[:, :], bank(2)[:, 0:SLOT_TILES], -1.0, None, ALU.add))
        mp = dve.mark(V.tensor_scalar(slots, bank(2)[:, 0:SLOT_TILES], 0.0, spare_row, ALU.is_equal, ALU.mult))
        dve.wait(m)
        m_gather = dve.mark(V.tensor_single_scalar(gather_i[:, :], gather_i[:, :], T - 1, ALU.bitwise_and))
        dve.wait(m1)
        m_at = dve.mark(V.tensor_copy(weights_at[:, :], bank(3)[:, 0:SLOT_TILES]))
        dve.wait(mp)
        m_scatter = dve.mark(V.scalar_tensor_tensor(scatter_u[:, :], bank(2)[:, 0:SLOT_TILES], -1.0, slots,
                                                    ALU.add, ALU.add))
        act.wait(m_diff[B - 1])
        m = act.mark(C.activation(wgt[:, :, 1], wgt[:, :, 1], ACT.Exp))
        dve.wait(m)
        m = dve.mark(V.tensor_scalar(wgt[:, :, 0], wgt[:, :, 1], 1.0, None, ALU.add))
        dve.wait(m)
        m = dve.mark(V.reciprocal(wgt[:, :, 0], wgt[:, :, 0]))
        dve.wait(m)
        m_wgt = dve.mark(V.tensor_tensor(wgt[:, :, 1], wgt[:, :, 1], wgt[:, :, 0], ALU.mult))
        C.preload_act_table_set("silu_and_others")

        flat_q = queries[:, :, :, :, :].rearrange("p b r j s -> p (b r j s)")
        XG, AHEAD = 8, 6
        c0 = [0]

        def ring(n, width):
            c0.append(c0[-1] + n * width)
            return flat_q[:, c0[-2]:c0[-1]]

        xg = ring(XG, 2 * D).rearrange("p (n c) -> p n c", n=XG)
        xT = ring(2, 2 * D).rearrange("p (n c) -> p n c", n=2)
        hs = ring(3, 2 * FF).rearrange("p (n i c) -> p n i c", n=3, i=2)
        hsT = ring(2, 2 * FF).rearrange("p (n i c) -> p n i c", n=2, i=2)
        sil = work[:, 0:2 * FF].rearrange("p (n c) -> p n c", n=2)
        hid = work[:, 2 * FF:4 * FF].rearrange("p (n c) -> p n c", n=2)
        y_slot = y_flat[:, 0:3 * D].rearrange("p (n d) -> p n d", n=3)
        all_weights = w_split[:, :, :].rearrange("p e n -> p (e n)")
        a_g, a_y = [arrivals(f"a_g{i}") for i in range(XG)], arrivals("a_y")
        fr, got_g, m_xT, m_sil, m_hid, m_hs, m_hsT, m_ys, at = ({} for _ in range(9))

        def gather(i):
            pool.wait(m_gather, fr.get(("xg", i % XG)), free["x2_split"], *attention_end)
            got_g[i] = a_g[i % XG].add(nc.gpsimd.indirect_dma_start(
                xg[:, i % XG, :].bitcast(F32), None, x2_dram[:, :],
                bass.IndirectOffsetOnAxis(ap=gather_i[:, i:i + 1].bitcast(U32), axis=0)))

        def turn_x2(i):
            pe.wait(got_g[i], fr.get("xbank"), m_cb, m_wgt)
            for h in range(2):
                m = pe.mark(TE.matmul(bank(6)[:, h * P:(h + 1) * P], xg[:, i % XG, h * D:(h + 1) * D], ident_r[:, :],
                                      start=True, stop=True))
            fr["xg", i % XG] = m
            act.wait(m, fr.get(("xT", i % 2)))
            m_xT[i] = fr["xbank"] = act.mark(C.activation(xT[:, i % 2, :], bank(6)[:, 0:2 * P], ACT.Identity))

        def expert_of(i):
            pe.wait(m_at)
            at[i] = TE.value_load(weights_at[0:1, i:i + 1], min_val=0, max_val=(NE - 1) * W_ALL)

        def up(i):
            s = i % 2
            pe.wait(m_xT[i], fr.get(("hbank", s)), m_split[PIECES - 1])
            for n, (xh, c) in enumerate(((0, W_HEAD), (0, W_REST), (1, W_HEAD))):
                for j in range(2):
                    m = pe.mark(TE.matmul(bank(2 * s + j), xT[:, i % 2, xh * P:(xh + 1) * P],
                                          all_weights[:, c + j * FF:][:, bass.ds(at[i], FF)], start=n == 0, stop=n == 2))
                if n == 1 and i + 1 < SLOT_TILES:
                    expert_of(i + 1)
            fr["xT", i % 2] = m
            act.wait(m, fr.get(("sil", s)))
            m_sil[i] = act.mark(C.activation(sil[:, s, :], bank(2 * s), ACT.Silu))
            dve.wait(m_sil[i], fr.get(("hid", s)))
            m_hid[i] = fr["hbank", s] = fr["sil", s] = dve.mark(V.tensor_tensor(
                hid[:, s, :], sil[:, s, :], bank(2 * s + 1), ALU.mult))

        def split_hidden(i):
            s, m = i % 2, m_hid[i]
            act.wait(m, fr.get(("hs", i % 3)))
            m1 = act.mark(C.activation(hs[:, i % 3, 0, :], hid[:, s, :], ACT.Identity))
            dve.wait(m1, m)
            m_hs[i] = fr["hid", s] = dve.mark(V.tensor_tensor(hs[:, i % 3, 1, :], hid[:, s, :],
                                                               hs[:, i % 3, 0, :].bitcast(F32), ALU.subtract))

        def turn_hidden(i):
            s = i % 2
            pe.wait(m_hs[i], fr.get("tbanks"))
            for h in range(2):
                for c in range(FC):
                    m = pe.mark(TE.matmul(bank(4 + h)[:, c * P:(c + 1) * P], hs[:, i % 3, h, c * P:(c + 1) * P], ident_r[:, :],
                                          start=True, stop=True))
                if h == 0:
                    act.wait(m, fr.get(("hsT", s)))
                    m1 = act.mark(C.activation(hsT[:, s, 0, :], bank(4), ACT.Identity))
            fr["hs", i % 3] = m
            dve.wait(m, fr.get(("hsT", s)))
            m2 = dve.mark(V.tensor_copy(hsT[:, s, 1, :], bank(5)))
            m_hsT[i] = fr["tbanks"] = [m1, m2]

        def down(i):
            s = i % 2
            yb = bank(7)
            pe.wait(m_hsT[i], fr.get("ybank"))
            for c in range(FC):
                w = all_weights[:, W_OUT + 2 * c * D:][:, bass.ds(at[i], 2 * D)]
                pe.mark(TE.matmul(yb[:, 0:2 * D], hsT[:, s, 0, c * P:(c + 1) * P], w, start=c == 0, stop=False))
                m = pe.mark(TE.matmul(yb[:, 0:D], hsT[:, s, 1, c * P:(c + 1) * P],
                                      all_weights[:, W_OUT + 2 * c * D:][:, bass.ds(at[i], D)],
                                      start=False, stop=c == FC - 1))
            fr["hsT", s] = m
            act.wait(m, fr.get("y_half"))
            m = act.mark(C.activation(y_half, yb[:, D:2 * D], ACT.Identity))
            dve.wait(m, fr.get(("y_slot", i % 3)))
            m = fr["ybank"] = fr["y_half"] = dve.mark(V.tensor_tensor(y_slot[:, i % 3, :], yb[:, 0:D], y_half, ALU.add))
            pool.wait(m, m_scatter, m_ys.get(i - 1))
            m_ys[i] = fr["y_slot", i % 3] = a_y.add(nc.gpsimd.indirect_dma_start(
                y_dram[:, :], bass.IndirectOffsetOnAxis(ap=scatter_u[:, i:i + 1], axis=0), y_slot[:, i % 3, :], None))

        for i in range(AHEAD):
            gather(i)
        turn_x2(0)
        expert_of(0)
        for i in range(SLOT_TILES + 2):
            if i + AHEAD < SLOT_TILES:
                gather(i + AHEAD)
            if i + 1 < SLOT_TILES:
                turn_x2(i + 1)
            if i < SLOT_TILES:
                up(i)
            if i >= 2:
                down(i - 2)
            if 1 <= i <= SLOT_TILES:
                turn_hidden(i - 1)
            if i < SLOT_TILES:
                split_hidden(i)

        C.preload_act_table_set("natural_log_exp_and_others")
        y_back = [x1[:, :, :], vals[:, :, :, :].rearrange("p t h d -> p (t h d)")[:, 0:NT * D].rearrange("p (t d) -> p t d", d=D)]
        a_b = [arrivals(f"a_b{g}") for g in range(4)]
        a_o = arrivals("a_o")
        ov = tiles(out)
        got_b = []
        for g in range(4):
            for k, line in enumerate((sp, act)):
                line.wait(m_ys[SLOT_TILES - 1])
                src = y_dram[k * T + g * 4 * P:k * T + (g + 1) * 4 * P].rearrange("(t p) d -> p t d", p=P)
                m = a_b[g].add(line.eng.dma_start(y_back[k][:, 4 * g:4 * g + 4, :], src))
            got_b.append(m)
        m_w0, m_w1 = [None] * 4, [None] * 4
        for g in range(4):
            sl = slice(4 * g, 4 * g + 4)
            act.wait(got_b[g], m_wgt)
            for t in range(4 * g, 4 * g + 4):
                m_w0[g] = act.mark(C.activation(y_back[0][:, t, :], y_back[0][:, t, :], ACT.Identity,
                                                scale=wgt[:, t, 0:1]))
            pool.wait(got_b[g], m_wgt)
            m_w1[g] = pool.mark(G.tensor_tensor(y_back[1][:, sl, :], y_back[1][:, sl, :],
                                                wgt[:, sl, 1:2].to_broadcast([P, 4, D]), ALU.mult))
        m_second = {}
        for g in (2, 3):
            sl = slice(4 * g, 4 * g + 4)
            pool.wait(m_w1[g])
            m_second[g] = pool.mark(G.tensor_tensor(x2[:, sl, :], x2[:, sl, :], y_back[1][:, sl, :], ALU.add))
        for half, line in ((0, pool), (1, dve)):
            for g in (2 * half, 2 * half + 1):
                tt, sl = range(4 * g, 4 * g + 4), slice(4 * g, 4 * g + 4)
                dve.wait(m_w0[g], m_second.get(g))
                m = dve.mark(V.tensor_tensor(x2[:, sl, :], x2[:, sl, :], y_back[0][:, sl, :], ALU.add))
                if half == 0:
                    dve.wait(m, m_w1[g])
                    m = dve.mark(V.tensor_tensor(x2[:, sl, :], x2[:, sl, :], y_back[1][:, sl, :], ALU.add))
                dve.wait(m)
                m = [dve.mark(V.bn_stats(stats[:, t, :], x2[:, t, :])) for t in tt][-1]
                dve.wait(m)
                m = [dve.mark(V.bn_aggr(mv[:, t, :], stats[:, t, :])) for t in tt][-1]
            hl = slice(8 * half, 8 * half + 8)
            dve.wait(m)
            m = rsqrt_exp(rstd[:, hl], mv[:, hl, 1], 1e-5, 1.0, rs_u[:, hl], rs_v[:, hl], m, line)
            line.wait(m)
            m = m_rstd = line.mark(line.eng.tensor_tensor(rs_u[:, hl], mv[:, hl, 0], rstd[:, hl], ALU.mult))
            line.wait(m)
            m_bias = line.mark(line.eng.tensor_scalar(rs_u[:, hl], rs_u[:, hl], -1.0, None, ALU.mult))
            for g in (2 * half, 2 * half + 1):
                tt, sl = range(4 * g, 4 * g + 4), slice(4 * g, 4 * g + 4)
                if g < 3:
                    act.wait(m_bias)
                    for t in tt:
                        m = act.mark(C.activation(x2[:, t, :], x2[:, t, :], ACT.Identity, scale=rstd[:, t:t + 1],
                                                  bias=rs_u[:, t:t + 1]))
                else:
                    dve.wait(m_rstd)
                    for t in tt:
                        m = dve.mark(V.tensor_scalar(x2[:, t, :], x2[:, t, :], mv[:, t, 0:1], rstd[:, t:t + 1],
                                                     ALU.subtract, ALU.mult))
                sp.wait(m)
                done = a_o.add(nc.sync.dma_start(ov[:, sl, :], x2[:, sl, :]))
        sp.wait(done)


def shape_constants():
    i = np.arange(P)
    same = np.ones((P, P))
    consts = np.concatenate([np.eye(P), i[:, None] <= i[None, :], i[:, None] > i[None, :], i[:, None] < i[None, :],
                             same * i[None, :], same * (i[:, None] // LT) * W_ALL,
                             i[:, None] + 1, PAIRS + 1 + i[:, None]], 1).astype(np.float32)
    inv = (1.0 / np.float32(10000.0) ** (np.arange(0, ROPE, 2, dtype=np.float32) / np.float32(ROPE))).astype(np.float32)
    ang = np.arange(S, dtype=np.float32)[:, None] * inv[None, :]
    cos, sin = np.cos(ang).astype(np.float32), np.sin(ang).astype(np.float32)
    cos = np.repeat(cos, 2, 1)
    sin = np.stack([-sin, sin], -1).reshape(S, ROPE)
    rope = np.stack([np.repeat(t.reshape(TPS, P, 1, ROPE), 2, 2).transpose(1, 0, 2, 3).reshape(P, -1) for t in (cos, sin)])
    return consts, np.ascontiguousarray(rope)


_INS = ["x", "ctx_1024", "L0_attn_ln_w", "L0_attn_ln_b", "L0_attn_W_in", "L0_attn_dt_bias", "L0_attn_A_log",
        "L0_attn_D", "L0_attn_W_out", "L0_xattn_bq", "L0_xattn_bk", "L0_xattn_bv", "L0_xattn_bo",
        "L0_ffn_gate_kernel", "L0_ffn_w0", "L0_ffn_w1", "L0_ffn_wo"]


def arrays_of(inputs):
    arrays = {n: np.ascontiguousarray(inputs[n]) for n in _INS}
    for n in "qkvo":
        arrays[f"w{n}T"] = np.ascontiguousarray(np.asarray(inputs[f"L0_xattn_W{n}"]).T)
    arrays["rms_w2"] = np.ascontiguousarray(np.asarray(inputs["L0_attn_rms_w"]).reshape(2, P).T)
    arrays["consts"], arrays["rope"] = shape_constants()
    return arrays


def kernel(**inputs):
    import concourse.bacc as bacc
    from concourse.bass_utils import run_bass_kernel_spmd

    nc = bacc.Bacc("TRN2", target_bir_lowering=False, num_devices=1)
    arrays = arrays_of(inputs)
    aps = {n: nc.dram_tensor(f"in_{n}", a.shape, F32, kind="ExternalInput").ap() for n, a in arrays.items()}
    out = nc.dram_tensor("out", (B, S, D), F32, kind="ExternalOutput").ap()
    build(nc, aps, out)
    r = run_bass_kernel_spmd(nc, [{f"in_{n}": a for n, a in arrays.items()}], core_ids=[0])
    return r.results[0]["out"]
```
